# Optimizing a Trainium2 kernel written in Bass

```python
import numpy as np
import jax
import jax.numpy as jnp

def _softmax(x, axis=-1):
    return jax.nn.softmax(x, axis=axis)

def _gelu(x):
    return jax.nn.gelu(x, approximate=True)

def _silu(x):
    return jax.nn.silu(x)

def _sigmoid(x):
    return jax.nn.sigmoid(x)

def _layernorm(x, axis=-1, eps=1e-05):
    m = jnp.mean(x, axis=axis, keepdims=True)
    v = jnp.var(x, axis=axis, keepdims=True)
    return (x - m) / jnp.sqrt(v + eps)

def _scatter_add(tgt, idx, src, axis=0):
    return tgt.at[idx].add(src)

def _segment_sum(src, seg, n):
    return jax.ops.segment_sum(src, seg, n)
kernel_name = 'mk_seq_postln_d2_jaxref_r8_59ee39'

def setup_inputs(seed: int=0):
    np.random.seed(seed)
    _w = jnp.asarray

    def _L0_attn_setup():
        import jax, jax.numpy as jnp
        import numpy as np
        D_MODEL = 256
        D_STATE = 64
        EXPAND = 2
        N_HEADS = 64
        NGROUPS = 1
        CHUNK = 32
        D_INNER = EXPAND * D_MODEL
        HEAD_DIM = D_INNER // N_HEADS
        BC = NGROUPS * D_STATE
        D_PROJ = 2 * D_INNER + 2 * BC + 2 * N_HEADS + D_STATE // 2
        SCALE = D_STATE ** (-0.5)
        EPS = 1e-06
        BATCH, T = (2, 256)

        def _rms_norm(x):
            return x * jax.lax.rsqrt(jnp.mean(x * x, axis=-1, keepdims=True) + EPS)

        def _rope_pairs(x, cos, sin):
            h = x.shape[-1] // 2
            x1, x2 = (x[..., :h], x[..., h:])
            return jnp.concatenate([x1 * cos - x2 * sin, x1 * sin + x2 * cos], axis=-1)

        def _segsum(v):
            L = v.shape[-1]
            cs = jnp.cumsum(v, axis=-1)
            d = cs[..., :, None] - cs[..., None, :]
            mask = jnp.tril(jnp.ones((L, L), dtype=bool))
            return jnp.where(mask, d, -jnp.inf)

        def _ssd_chunked(x, A, Bm, Cm, dt):
            b, Tt, H, P = x.shape
            rep = H // NGROUPS
            Bh = jnp.repeat(Bm, rep, axis=2)
            Ch = jnp.repeat(Cm, rep, axis=2) * SCALE
            c = Tt // CHUNK
            xd = (x * dt[..., None]).reshape(b, c, CHUNK, H, P)
            Bh = Bh.reshape(b, c, CHUNK, H, D_STATE)
            Ch = Ch.reshape(b, c, CHUNK, H, D_STATE)
            dA = (dt * A).reshape(b, c, CHUNK, H)
            Acs = jnp.cumsum(dA, axis=2)
            Lm = jnp.exp(_segsum(jnp.moveaxis(dA, 3, 2)))
            Y_diag = jnp.einsum('bclhn,bcshn,bchls,bcshp->bclhp', Ch, Bh, Lm, xd)
            decay_states = jnp.exp(Acs[:, :, -1:, :] - Acs)
            states = jnp.einsum('bclhn,bclh,bclhp->bchpn', Bh, decay_states, xd)
            chunk_decay = jnp.exp(Acs[:, :, -1])

            def step(h, inp):
                dec, s = inp
                return (h * dec[:, :, None, None] + s, h)
            h0 = jnp.zeros((b, H, P, D_STATE), x.dtype)
            _, prev = jax.lax.scan(step, h0, (jnp.moveaxis(chunk_decay, 1, 0), jnp.moveaxis(states, 1, 0)))
            prev = jnp.moveaxis(prev, 0, 1)
            Y_off = jnp.einsum('bclhn,bchpn,bclh->bclhp', Ch, prev, jnp.exp(Acs))
            return (Y_diag + Y_off).reshape(b, Tt, H, P)
        key = jax.random.key(seed)
        k = jax.random.split(key, 4)
        x = jax.random.normal(k[0], (BATCH, T, D_MODEL), dtype=jnp.float32)
        W_in = jax.random.normal(k[1], (D_MODEL, D_PROJ), dtype=jnp.float32) * D_MODEL ** (-0.5)
        W_out = jax.random.normal(k[2], (D_INNER, D_MODEL), dtype=jnp.float32) * D_INNER ** (-0.5)
        A_log = jnp.zeros((N_HEADS,), jnp.float32)
        dt_bias = jnp.zeros((N_HEADS,), jnp.float32)
        B_norm_bias = jnp.ones((NGROUPS, D_STATE), jnp.float32)
        C_norm_bias = jnp.ones((NGROUPS, D_STATE), jnp.float32)
        return {'x': x, 'W_in': W_in, 'A_log': A_log, 'dt_bias': dt_bias, 'B_norm_bias': B_norm_bias, 'C_norm_bias': C_norm_bias, 'W_out': W_out}
    _L0_attn_in = _L0_attn_setup()

    def _L0_ffn_setup():
        import jax, jax.numpy as jnp
        import numpy as np
        DIM = 256
        HID = 704
        ZERO_POINT = 128.0

        def _qlinear(x, wq, scale):
            W = (wq.astype(jnp.float32) - ZERO_POINT) * scale[:, None]
            return jnp.einsum('bsd,hd->bsh', x, W)
        key = jax.random.key(seed)
        ks = jax.random.split(key, 7)
        B, S = (4, 256)
        sg = jax.random.uniform(ks[1], (HID,)) * (0.02 / np.sqrt(DIM)) + 0.0001
        su = jax.random.uniform(ks[3], (HID,)) * (0.02 / np.sqrt(DIM)) + 0.0001
        sd = jax.random.uniform(ks[5], (DIM,)) * (0.02 / np.sqrt(HID)) + 0.0001
        return {'x': jax.random.normal(ks[0], (B, S, DIM), dtype=jnp.float32), 'wq_gate': jax.random.randint(ks[2], (HID, DIM), 0, 32, dtype=jnp.int32), 's_gate': sg, 'wq_up': jax.random.randint(ks[4], (HID, DIM), 0, 32, dtype=jnp.int32), 's_up': su, 'wq_down': jax.random.randint(ks[6], (DIM, HID), 0, 32, dtype=jnp.int32), 's_down': sd}
    _L0_ffn_in = _L0_ffn_setup()

    def _L1_attn_setup():
        import jax, jax.numpy as jnp
        import numpy as np
        EPS = 1.1920929e-07

        def _rms(x):
            return x * jax.lax.rsqrt(jnp.mean(x * x, axis=-1, keepdims=True) + EPS)
        key = jax.random.key(seed)
        k0, k1, k2, k3 = jax.random.split(key, 4)
        B, S, D, DFF = (4, 256, 256, 1024)
        x = jax.random.normal(k0, (B, S, D), dtype=jnp.float32)
        w_qkv = jax.random.normal(k1, (3 * D, D), dtype=jnp.float32) * 0.02
        w_swiglu = jax.random.normal(k2, (2 * DFF, D), dtype=jnp.float32) * 0.02
        w_out = jax.random.normal(k3, (D, DFF), dtype=jnp.float32) * 0.02
        return {'x': x, 'w_qkv': w_qkv, 'w_swiglu': w_swiglu, 'w_out': w_out}
    _L1_attn_in = _L1_attn_setup()

    def _L1_ffn_setup():
        import jax, jax.numpy as jnp
        import numpy as np
        E, K = (16, 4)
        C, H = (256, 448)
        B, T = (2, 64)
        STD = 0.02
        key = jax.random.key(seed)
        ks = jax.random.split(key, 5)
        x = jax.random.normal(ks[0], (B, T, C), jnp.float32)
        W_up = jax.random.normal(ks[1], (E, H, C), jnp.float32) * STD
        W_gate = jax.random.normal(ks[2], (E, H, C), jnp.float32) * STD
        W_down = jax.random.normal(ks[3], (E, C, H), jnp.float32) * STD
        gate_inp = jax.random.normal(ks[4], (E, C), jnp.float32) * STD
        return {'x': x, 'W_up': W_up, 'W_gate': W_gate, 'W_down': W_down, 'gate_inp': gate_inp}
    _L1_ffn_in = _L1_ffn_setup()
    _d = {'L0_attn_x': _L0_attn_in['x'], 'L0_attn_W_in': _L0_attn_in['W_in'], 'L0_attn_A_log': _L0_attn_in['A_log'], 'L0_attn_dt_bias': _L0_attn_in['dt_bias'], 'L0_attn_B_norm_bias': _L0_attn_in['B_norm_bias'], 'L0_attn_C_norm_bias': _L0_attn_in['C_norm_bias'], 'L0_attn_W_out': _L0_attn_in['W_out'], 'L0_ffn_wq_gate': _L0_ffn_in['wq_gate'], 'L0_ffn_s_gate': _L0_ffn_in['s_gate'], 'L0_ffn_wq_up': _L0_ffn_in['wq_up'], 'L0_ffn_s_up': _L0_ffn_in['s_up'], 'L0_ffn_wq_down': _L0_ffn_in['wq_down'], 'L0_ffn_s_down': _L0_ffn_in['s_down'], 'L1_attn_w_qkv': _L1_attn_in['w_qkv'], 'L1_attn_w_swiglu': _L1_attn_in['w_swiglu'], 'L1_attn_w_out': _L1_attn_in['w_out'], 'L1_ffn_W_up': _L1_ffn_in['W_up'], 'L1_ffn_W_gate': _L1_ffn_in['W_gate'], 'L1_ffn_W_down': _L1_ffn_in['W_down'], 'L1_ffn_gate_inp': _L1_ffn_in['gate_inp']}
    _x0 = _d['L0_attn_x']
    _d['L0_attn_x'] = jax.random.normal(jax.random.fold_in(jax.random.key(seed), 1), (16, 256, 256), dtype=_x0.dtype)
    del _x0
    return _d

def reference(L0_attn_x, L0_attn_W_in, L0_attn_A_log, L0_attn_dt_bias, L0_attn_B_norm_bias, L0_attn_C_norm_bias, L0_attn_W_out, L0_ffn_wq_gate, L0_ffn_s_gate, L0_ffn_wq_up, L0_ffn_s_up, L0_ffn_wq_down, L0_ffn_s_down, L1_attn_w_qkv, L1_attn_w_swiglu, L1_attn_w_out, L1_ffn_W_up, L1_ffn_W_gate, L1_ffn_W_down, L1_ffn_gate_inp):

    def _L0_attn_ref(x, W_in, A_log, dt_bias, B_norm_bias, C_norm_bias, W_out):
        import jax, jax.numpy as jnp
        import numpy as np
        D_MODEL = 256
        D_STATE = 64
        EXPAND = 2
        N_HEADS = 64
        NGROUPS = 1
        CHUNK = 32
        D_INNER = EXPAND * D_MODEL
        HEAD_DIM = D_INNER // N_HEADS
        BC = NGROUPS * D_STATE
        D_PROJ = 2 * D_INNER + 2 * BC + 2 * N_HEADS + D_STATE // 2
        SCALE = D_STATE ** (-0.5)
        EPS = 1e-06
        BATCH, T = (2, 256)

        def _rms_norm(x):
            return x * jax.lax.rsqrt(jnp.mean(x * x, axis=-1, keepdims=True) + EPS)

        def _rope_pairs(x, cos, sin):
            h = x.shape[-1] // 2
            x1, x2 = (x[..., :h], x[..., h:])
            return jnp.concatenate([x1 * cos - x2 * sin, x1 * sin + x2 * cos], axis=-1)

        def _segsum(v):
            L = v.shape[-1]
            cs = jnp.cumsum(v, axis=-1)
            d = cs[..., :, None] - cs[..., None, :]
            mask = jnp.tril(jnp.ones((L, L), dtype=bool))
            return jnp.where(mask, d, -jnp.inf)

        def _ssd_chunked(x, A, Bm, Cm, dt):
            b, Tt, H, P = x.shape
            rep = H // NGROUPS
            Bh = jnp.repeat(Bm, rep, axis=2)
            Ch = jnp.repeat(Cm, rep, axis=2) * SCALE
            c = Tt // CHUNK
            xd = (x * dt[..., None]).reshape(b, c, CHUNK, H, P)
            Bh = Bh.reshape(b, c, CHUNK, H, D_STATE)
            Ch = Ch.reshape(b, c, CHUNK, H, D_STATE)
            dA = (dt * A).reshape(b, c, CHUNK, H)
            Acs = jnp.cumsum(dA, axis=2)
            Lm = jnp.exp(_segsum(jnp.moveaxis(dA, 3, 2)))
            Y_diag = jnp.einsum('bclhn,bcshn,bchls,bcshp->bclhp', Ch, Bh, Lm, xd)
            decay_states = jnp.exp(Acs[:, :, -1:, :] - Acs)
            states = jnp.einsum('bclhn,bclh,bclhp->bchpn', Bh, decay_states, xd)
            chunk_decay = jnp.exp(Acs[:, :, -1])

            def step(h, inp):
                dec, s = inp
                return (h * dec[:, :, None, None] + s, h)
            h0 = jnp.zeros((b, H, P, D_STATE), x.dtype)
            _, prev = jax.lax.scan(step, h0, (jnp.moveaxis(chunk_decay, 1, 0), jnp.moveaxis(states, 1, 0)))
            prev = jnp.moveaxis(prev, 0, 1)
            Y_off = jnp.einsum('bclhn,bchpn,bclh->bclhp', Ch, prev, jnp.exp(Acs))
            return (Y_diag + Y_off).reshape(b, Tt, H, P)
        b, Tt, _ = x.shape
        proj = x @ W_in
        d, bc, nh = (D_INNER, BC, N_HEADS)
        z = proj[..., :d]
        x_raw = proj[..., d:2 * d]
        B_mat = proj[..., 2 * d:2 * d + bc].reshape(b, Tt, NGROUPS, D_STATE)
        C_mat = proj[..., 2 * d + bc:2 * d + 2 * bc].reshape(b, Tt, NGROUPS, D_STATE)
        dt_raw = proj[..., 2 * d + 2 * bc:2 * d + 2 * bc + nh]
        lambda_raw = proj[..., 2 * d + 2 * bc + nh:2 * d + 2 * bc + 2 * nh]
        theta_raw = proj[..., 2 * d + 2 * bc + 2 * nh:]
        x_raw = jax.nn.silu(x_raw)
        B_mat = _rms_norm(B_mat) * B_norm_bias
        C_mat = _rms_norm(C_mat) * C_norm_bias
        A = -jnp.exp(A_log)
        dt = jnp.clip(jax.nn.softplus(dt_raw + dt_bias), 0.0001, 0.5)
        dt_mean = jnp.mean(dt, axis=-1, keepdims=True)
        cum = -jnp.cumsum(dt_mean * theta_raw, axis=1)
        cos = jnp.cos(cum)[:, :, None, :]
        sin = jnp.sin(cum)[:, :, None, :]
        B_mat = _rope_pairs(B_mat, cos, sin)
        C_mat = _rope_pairs(C_mat, cos, sin)
        xh = x_raw.reshape(b, Tt, N_HEADS, HEAD_DIM)
        lam = jax.nn.sigmoid(lambda_raw)
        alpha = jnp.exp(A * dt)
        x_gamma = xh * lam[..., None]
        x_shift = jnp.pad(xh[:, :-1], ((0, 0), (1, 0), (0, 0), (0, 0)))
        x_beta = x_shift * ((1.0 - lam) * alpha)[..., None]
        B_shift = jnp.pad(B_mat[:, :-1], ((0, 0), (1, 0), (0, 0), (0, 0)))
        y = _ssd_chunked(x_gamma, A, B_mat, C_mat, dt) + _ssd_chunked(x_beta, A, B_shift, C_mat, dt)
        y = y.reshape(b, Tt, D_INNER)
        y = _rms_norm(y) * jax.nn.silu(z)
        return y @ W_out

    def _L0_ffn_ref(x, wq_gate, s_gate, wq_up, s_up, wq_down, s_down):
        import jax, jax.numpy as jnp
        import numpy as np
        DIM = 256
        HID = 704
        ZERO_POINT = 128.0

        def _qlinear(x, wq, scale):
            W = (wq.astype(jnp.float32) - ZERO_POINT) * scale[:, None]
            return jnp.einsum('bsd,hd->bsh', x, W)
        gate = _qlinear(x, wq_gate, s_gate)
        gate = jax.nn.silu(gate)
        up = _qlinear(x, wq_up, s_up)
        return _qlinear(gate * up, wq_down, s_down)

    def _L1_attn_ref(x, w_qkv, w_swiglu, w_out):
        import jax, jax.numpy as jnp
        import numpy as np
        EPS = 1.1920929e-07

        def _rms(x):
            return x * jax.lax.rsqrt(jnp.mean(x * x, axis=-1, keepdims=True) + EPS)
        qkv = _rms(x) @ w_qkv.T
        q, k, v = jnp.split(qkv, 3, axis=-1)
        q = _rms(q)
        k = _rms(k)
        w = jnp.exp(k)
        kv_cum = jnp.cumsum(w * v, axis=1)
        w_cum = jnp.cumsum(w, axis=1)
        y = jax.nn.sigmoid(q) * (kv_cum / (w_cum + 1e-06))
        uv = y @ w_swiglu.T
        u, g = jnp.split(uv, 2, axis=-1)
        return x + u * jax.nn.silu(g) @ w_out.T

    def _L1_ffn_ref(x, W_up, W_gate, W_down, gate_inp):
        import jax, jax.numpy as jnp
        import numpy as np
        E, K = (16, 4)
        C, H = (256, 448)
        B, T = (2, 64)
        STD = 0.02
        b, t, c = x.shape
        xf = x.reshape(b * t, c)
        logits = xf @ gate_inp.T
        topv, topi = jax.lax.top_k(logits, K)
        w = jax.nn.softmax(topv.astype(jnp.float32), axis=-1).astype(x.dtype)
        n = xf.shape[0]
        dense_w = jnp.zeros((n, E), x.dtype).at[jnp.arange(n)[:, None], topi].set(w)
        u = jnp.einsum('nc,ehc->neh', xf, W_up)
        g = jnp.einsum('nc,ehc->neh', xf, W_gate)
        h = jax.nn.silu(g) * u
        y = jnp.einsum('neh,ech,ne->nc', h, W_down, dense_w)
        return y.reshape(b, t, c)
    x = L0_attn_x
    x = _layernorm(x + _L0_attn_ref(x, L0_attn_W_in, L0_attn_A_log, L0_attn_dt_bias, L0_attn_B_norm_bias, L0_attn_C_norm_bias, L0_attn_W_out), axis=-1)
    x = _layernorm(x + _L0_ffn_ref(x, L0_ffn_wq_gate, L0_ffn_s_gate, L0_ffn_wq_up, L0_ffn_s_up, L0_ffn_wq_down, L0_ffn_s_down), axis=-1)
    x = _layernorm(x + _L1_attn_ref(x, L1_attn_w_qkv, L1_attn_w_swiglu, L1_attn_w_out), axis=-1)
    x = _layernorm(x + _L1_ffn_ref(x, L1_ffn_W_up, L1_ffn_W_gate, L1_ffn_W_down, L1_ffn_gate_inp), axis=-1)
    return x

_drawn_inputs = setup_inputs


def setup_inputs(seed=0):
    import zlib

    import numpy as np

    out = dict(_drawn_inputs(seed))
    spreads = {'L0_attn_A_log': (0.0, 0.1),
     'L0_attn_dt_bias': (0.0, 0.638),
     'L0_attn_B_norm_bias': (1.0, 0.2),
     'L0_attn_C_norm_bias': (1.0, 0.2)}
    factors = {'L0_ffn_s_gate': 8.0,
     'L0_ffn_s_up': 8.0,
     'L0_ffn_s_down': 8.0,
     'L1_attn_w_qkv': 8.0,
     'L1_attn_w_swiglu': 8.0,
     'L1_attn_w_out': 8.0,
     'L1_ffn_W_up': 4.958,
     'L1_ffn_W_gate': 5.001,
     'L1_ffn_W_down': 4.922,
     'L1_ffn_gate_inp': 5.655}
    for name, (base, spread) in spreads.items():
        noise = np.random.default_rng([zlib.crc32(name.encode()), seed]).standard_normal(out[name].shape)
        drawn = base * np.exp(spread * noise) if base else spread * noise
        out[name] = jnp.asarray(drawn.astype(out[name].dtype))
    for name, factor in factors.items():
        out[name] = (out[name] * factor).astype(out[name].dtype)
    return out
```

```python
from contextlib import ExitStack

import numpy as np

import concourse.bass as bass
from concourse import mybir

F32 = mybir.dt.float32
BF16 = mybir.dt.bfloat16
I32 = mybir.dt.int32
U32 = mybir.dt.uint32
ALU = mybir.AluOpType
ACT = mybir.ActivationFunctionType
AX_X = mybir.AxisListType.X

P = 128
T = 256
NT = T // P
D = 256
DC = D // P
DI = 512
H = 64
HD = DI // H
N = 64
REST = 2 * N + 2 * H + N // 2
LV = 7
FH = 704
FJ = (FH + P - 1) // P
SH = 1024
SJ = SH // P
NE = 16
TOPK = 4
EH = 448
EC = 112
EJ = EH // EC
UN = 8
MAGIC = 1.5 * 2.0 ** 23
TWO_PI_HI = 6.28125
TWO_PI_LO = 2.0 * np.pi - 6.28125
DT_MIN, DT_MAX = 0.0001, 0.5
DVE_A, DVE_B = 20, 17

SUFFIX, PREFIX, STRICT, ONES, SHIFT, EDGE, IDENT = range(LV, LV + 7)
MASK0 = LV + 7


def constant_matrices():
    r, c = np.arange(P)[:, None], np.arange(P)[None, :]
    m = np.zeros((P, MASK0 + LV, P), np.float32)
    for k in range(LV):
        half = 2 ** k
        same = r // (2 * half) == c // (2 * half)
        right_r, right_c = r // half % 2 == 1, c // half % 2 == 1
        m[:, k] = same & np.where(right_c, right_r & (r <= c), ~right_r & (r > c))
        m[:, MASK0 + k] = same & ~right_r & right_c
    m[:, SUFFIX] = r > c
    m[:, PREFIX] = r <= c
    m[:, STRICT] = r < c
    m[:, ONES] = 1
    m[:, SHIFT] = r == c + 1
    m[:, EDGE] = (r == 0) & (c == P - 1)
    m[:, IDENT] = r == c
    return m


def tile_count(tokens):
    most = (tokens * TOPK + NE * (P - 1) + NE - 1) // P
    return -(-most // UN) * UN


class Signal:

    def __init__(self, sem, per):
        self.sem, self.per = sem, per

    def at(self, s, k=None):
        return s * self.per + (self.per if k is None else k)

    def before(self, s):
        return s * self.per


def later(s, n=1):
    return not isinstance(s, int) or s >= n


class Carrier:

    def __init__(self, eng, sem):
        self.eng, self.sem = eng, sem

    def take(self):
        self.eng.sem_inc(self.sem, 1)


class Chain:

    def __init__(self, eng, sem, per):
        self.eng, self.sem, self.per, self.k, self.s = eng, sem, per, 0, 0

    def start(self, s):
        self.s, self.k = s, 0

    def go_on(self, s):
        self.s = s

    def step(self, ins):
        self.k += 1
        ins.then_inc(self.sem, 1)
        self.eng.wait_ge(self.sem, self.s * self.per + self.k)

    def end(self):
        assert self.k == self.per, (self.k, self.per)


def spread(ap, axis, n):
    a = ap.unsqueeze(axis)
    shape = list(a.shape)
    shape[axis] = n
    return a.broadcast_to(shape)


ORDER = (["B1", "C8", "A2", "B2", "A3", "A4.0", "F0", "B2L", "A4.1", "A4.2", "A4.3", "B3", "A4.4", "A4.5"]
         + ["B4", "A4.6", "A4.7", "B5.0", "B5.1", "B5.2", "B5.3", "B5.4", "A5", "B5.5", "B5.6", "B5.7"]
         + ["A6", "B6", "F1", "F2", "F3", "B7"])
SHIFT_OF = {"F": 1, "A": 0, "B": -1, "C": -2}


def run_skewed(eng, nseq, pieces):

    def one_round(i):
        for name in ORDER:
            s = i + SHIFT_OF[name[0]]
            whole, _, k = name.partition(".")
            if whole in pieces and (not isinstance(i, int) or 0 <= s < nseq):
                pieces[whole](s, *([int(k)] if k else []))

    first, end = 2, max(2, nseq - 1)
    for i in range(-1, first):
        one_round(i)
    if end > first:
        with eng.Fori(first, end) as i:
            one_round(i)
    for i in range(end, nseq + 2):
        one_round(i)


def build(nc, ins, out):
    nseq = ins["x"].shape[0] // T
    ntok = nseq * T
    cap = ntok + P
    ntile = tile_count(ntok)
    nslot = (NE + 1) * cap

    meta_dram = nc.dram_tensor("meta_dram", [nslot, 4], U32).ap()
    x3_dram = nc.dram_tensor("x3_dram", [ntok, D], F32).ap()
    yk_dram = nc.dram_tensor("yk_dram", [ntok * TOPK, D], F32).ap()

    with ExitStack() as whole:
        ident = whole.enter_context(nc.sbuf_tensor("ident", [P, P], F32))
        small = whole.enter_context(nc.sbuf_tensor("small", [P, ins["small"].shape[1]], F32))
        base = whole.enter_context(nc.sbuf_tensor("base", [P, NE], F32))
        layers_block(nc, ins, nseq, cap, ident, small, base, meta_dram, x3_dram)
        experts_block(nc, ins, ntok, cap, ntile, ident, small, base, meta_dram, x3_dram, yk_dram)
        combine_block(nc, nseq, x3_dram, yk_dram, out)


SM_P, SM_E, SM_DST, SM_TRI, SM_I = 0, 1, 1 + NE, 1 + NE + NT * TOPK, 1 + NE + NT * TOPK + NE * NE


def small_constants(ntile):
    s = np.zeros((P, SM_I + ntile), np.float32)
    p = np.arange(P)
    s[:, SM_P] = p
    s[:, SM_E:SM_DST] = np.arange(NE)
    dst = (np.arange(NT)[None, :, None] * P + p[:, None, None]) * TOPK + np.arange(TOPK)[None, None, :]
    s[:, SM_DST:SM_TRI] = dst.reshape(P, -1)
    s[:, SM_TRI:SM_I] = np.tril(np.ones((NE, NE))).reshape(1, -1)
    s[:, SM_I:] = np.arange(ntile)
    return s


def layers_block(nc, ins, nseq, cap, ident, small, base, meta_dram, x3_dram):
    with ExitStack() as ctx:
        def sb(name, shape, dt=F32):
            return ctx.enter_context(nc.sbuf_tensor(name, shape, dt))

        def sig(name, per):
            return Signal(ctx.enter_context(nc.semaphore(name)), per)

        const = sb("const", [P, MASK0 + LV, P])
        w_in = sb("w_in", [P, DC, 2 * DI + REST])
        w_out = sb("w_out", [P, DI // P, D])
        w_gate = sb("w_gate", [P, DC, FH])
        w_up = sb("w_up", [P, DC, FH])
        w_down = sb("w_down", [P, FJ, D])
        s_gu = sb("s_gu", [P, 2, FJ])
        s_down = sb("s_down", [P, D])
        w_qkv = sb("w_qkv", [P, DC, 3 * D])
        w_sw = sb("w_sw", [P, DC, 2 * SH])
        w_so = sb("w_so", [P, SJ, D])
        w_route = sb("w_route", [P, DC, NE])
        dt_bias = sb("dt_bias", [P, H])
        neg_a = sb("neg_a", [P, H])
        bc_bias = sb("bc_bias", [P, 2, N])

        xT = sb("xT", [P, DC, T])
        x_row = sb("x_row", [P, NT, D])
        rest = sb("rest", [P, NT, REST])
        xs = sb("xs", [P, NT, DI])
        zs = sb("zs", [P, NT, DI])
        vl = sb("vl", [P, NT, 2 * H])
        eu = sb("eu", [P, NT, 2 * H])
        rec = sb("rec", [P, NT, 2 * H])
        lnw = sb("lnw", [P, NT, H])
        dt = sb("dt", [P, NT, H])
        d_a = sb("d_a", [P, NT, H])
        ld = sb("ld", [P, NT, H])
        q = sb("q", [P, NT, H])
        g = sb("g", [P, NT, H])
        coef = sb("coef", [P, NT, H])
        dtm = sb("dtm", [P, NT])
        power = sb("power", [P, 4])
        dth = sb("dth", [P, NT, N // 2])
        bcn = sb("bcn", [P, NT, 2, N])
        bct = sb("bct", [P, NT, 2, N])
        bcu = sb("bcu", [P, NT, 2, N])
        bcr = sb("bcr", [P, NT, 2, N])
        ssq = sb("ssq", [P, NT, 2])
        ang = sb("ang", [P, NT, 2, N // 2])
        turns = sb("turns", [P, NT, 2, N // 2])
        cs = sb("cs", [P, NT, 2, N // 2])
        cb = sb("cb", [P, NT])
        bcT = sb("bcT", [N, NT, 2, P])
        decay = sb("decay", [P, LV + 1, NT, H])
        masked = sb("masked", [P, NT, LV, P])
        cross = sb("cross", [P, P])
        xg = sb("xg", [P, NT, DI])
        u = sb("u", [P, 2, NT, DI])
        v = sb("v", [P, 2, NT, DI])
        y = sb("y", [P, NT, DI])
        ynT = sb("ynT", [P, NT, DI // P, P])
        sq_a = sb("sq_a", [P, DI])
        yss = sb("yss", [P, NT])
        r1 = sb("r1", [P, NT, D])
        st1 = sb("st1", [P, NT, 6])
        mv1 = sb("mv1", [P, NT, 2])

        x1 = sb("x1", [P, NT, D])
        x1T = sb("x1T", [P, DC, T])
        sg = sb("sg", [P, 2, T])
        hT = sb("hT", [P, SJ, T])
        x2 = sb("x2", [P, NT, D])
        r2 = sb("r2", [P, NT, D])
        st2 = sb("st2", [P, NT, 6])
        mv2 = sb("mv2", [P, NT, 2])
        x2n = sb("x2n", [P, NT, D])
        sq_b = sb("sq_b", [P, D])
        rss = sb("rss", [P, NT])
        qk_ss = sb("qk_ss", [P, NT, 2])
        eq = sb("eq", [P, NT, D])
        wv = sb("wv", [P, NT, 2, D])
        den = sb("den", [P, NT, D])
        yc = sb("yc", [P, NT, D])
        x3 = sb("x3", [P, NT, D])
        logits = sb("logits", [P, NT, NE])
        top = sb("top", [P, NT, 8])
        topi = sb("topi", [P, NT, 8], U32)
        topf = sb("topf", [P, NT, TOPK])
        ez = sb("ez", [P, NT, TOPK])
        esum = sb("esum", [P, NT])
        hot = sb("hot", [P, NT, TOPK, NE])
        hot_pos = sb("hot_pos", [P, NT, TOPK, NE])
        chosen = sb("chosen", [P, NT, NE])
        pos = sb("pos", [P, NT, NE])
        slot_f = sb("slot_f", [P, NT, TOPK])
        slot = sb("slot", [P, NT, TOPK], U32)
        dst = sb("dst", [P, NT, TOPK])
        tok = sb("tok", [P, NT])
        meta = sb("meta", [P, NT, TOPK, 4], U32)

        pa = ctx.enter_context(nc.psum_tensor("pa", [P, 4, 512], F32))
        pb = ctx.enter_context(nc.psum_tensor("pb", [P, 4, 512], F32))
        ident = ident[:, :]

        def mat(k):
            return const[:, k, :]

        loads = [(const[:, :, :], ins["matrices"]), (ident, ins["matrices"][:, IDENT, :]), (small[:, :], ins["small"]),
                 (w_in[:, :, :], ins["w_in"].rearrange("(c p) n -> p c n", p=P)),
                 (dt_bias[:, :], ins["dt_bias"]), (neg_a[:, :], ins["a_log"]),
                 (bc_bias[:, :, :], ins["bc_bias"]),
                 (w_out[:, :, :], ins["w_out"].rearrange("(c p) n -> p c n", p=P))]
        loads_b = [(w_gate[:, :, :].bitcast(I32), ins["w_gate"].rearrange("(c p) n -> p c n", p=P)),
                   (w_up[:, :, :].bitcast(I32), ins["w_up"].rearrange("(c p) n -> p c n", p=P)),
                   (w_down[:, 0:FJ - 1, :].bitcast(I32),
                    ins["w_down"][0:(FJ - 1) * P, :].rearrange("(c p) n -> p c n", p=P)),
                   (w_down[0:FH - (FJ - 1) * P, FJ - 1, :].bitcast(I32), ins["w_down"][(FJ - 1) * P:FH, :]),
                   (s_gu[:, :, :], ins["s_gu"]), (s_down[:, :], ins["s_down"]),
                   (w_qkv[:, :, :], ins["w_qkv"].rearrange("(c p) n -> p c n", p=P)),
                   (w_sw[:, :, :], ins["w_sw"].rearrange("(c p) n -> p c n", p=P)),
                   (w_so[:, :, :], ins["w_so"].rearrange("(c p) n -> p c n", p=P)),
                   (w_route[:, :, :], ins["w_route"].rearrange("(c p) n -> p c n", p=P))]
        setup_loaded = sig("setup_loaded", 16 * len(loads))
        weights_loaded = sig("weights_loaded", 16 * len(loads_b))
        dequantised = sig("dequantised", 4)
        setup_done = sig("setup_done", 1)
        a_exp = sig("a_exp", 1)

        xT_in = sig("xT_in", 16)
        x_row_in = sig("x_row_in", 16)
        rest_projected = sig("rest_projected", NT)
        x_projected = sig("x_projected", NT)
        z_projected = sig("z_projected", NT)
        rest_copied = sig("rest_copied", NT)
        xs_ready = sig("xs_ready", NT)
        zs_ready = sig("zs_ready", NT)
        v_ready = sig("v_ready", 1)
        eu_ready = sig("eu_ready", 1)
        w_ready = sig("w_ready", 1)
        ln_ready = sig("ln_ready", 1)
        steps_ready = sig("steps_ready", 1)
        shifted = sig("shifted", 1)
        decay_sums = sig("decay_sums", 1)
        decay_ready = sig("decay_ready", 1)
        ang_ready = sig("ang_ready", 1)
        sin_ready = sig("sin_ready", 1)
        g_ready = sig("g_ready", 1)
        roped = sig("roped", 1)
        coef_ready = sig("coef_ready", 1)
        bc_transposed = sig("bc_transposed", 1)
        bcT_ready = sig("bcT_ready", 1)
        cb_ready = sig("cb_ready", 1)
        masked_ready = sig("masked_ready", NT)
        cross_ready = sig("cross_ready", 1)
        xg_ready = sig("xg_ready", 1)
        u_ready = sig("u_ready", LV + 1)
        level_done = sig("level_done", LV + 1)
        v_scaled = sig("v_scaled", LV + 1)
        y_added = sig("y_added", LV + 2)
        yss_ready = sig("yss_ready", NT)
        yn_ready = sig("yn_ready", NT)
        yn_transposed = sig("yn_transposed", NT)
        ynT_ready = sig("ynT_ready", NT)
        out_projected = sig("out_projected", 1)
        x1_ready = sig("x1_ready", NT)
        bc_squares, bc_rms, y_rms, x2_rms = (sig(n, 1) for n in ("bc_squares", "bc_rms", "y_rms", "x2_rms"))
        norm1, norm2, norm3 = ((sig(f"variance{n}", 1), sig(f"deviation{n}", 1)) for n in (1, 2, 3))
        power_set = sig("power_set", 1)
        pool_waited, dve_waited, pe_waited = (ctx.enter_context(nc.semaphore(f"{n}_waited")) for n in ("pool", "dve", "pe"))
        pool_a = sig("pool_a", 3)
        pool_b = sig("pool_b", 5)
        dve_a = sig("dve_a", DVE_A)

        x1_transposed = sig("x1_transposed", 1)
        x1T_ready = sig("x1T_ready", 1)
        ffn_projected = sig("ffn_projected", FJ)
        ffn_silu = sig("ffn_silu", FJ)
        ffn_h = sig("ffn_h", FJ)
        ffn_out = sig("ffn_out", 1)
        x2_ready = sig("x2_ready", NT)
        rss_ready = sig("rss_ready", NT)
        x2n_ready = sig("x2n_ready", NT)
        x2_transposed = sig("x2_transposed", 1)
        x2T_ready = sig("x2T_ready", 1)
        qk_projected = sig("qk_projected", NT)
        v_projected = sig("v_projected", 1)
        qk_ss_ready = sig("qk_ss_ready", NT * 2)
        qk_rms_ready = sig("qk_rms_ready", 1)
        k_exp = sig("k_exp", NT)
        q_exp = sig("q_exp", NT)
        wv_ready = sig("wv_ready", NT)
        cumulated = sig("cumulated", NT)
        yc_ready = sig("yc_ready", 1)
        yc_transposed = sig("yc_transposed", 1)
        ycT_ready = sig("ycT_ready", 1)
        sw_projected = sig("sw_projected", SJ)
        sw_silu = sig("sw_silu", SJ)
        sw_h = sig("sw_h", SJ)
        sw_out = sig("sw_out", 1)
        x3_ready = sig("x3_ready", NT)
        x3_transposed = sig("x3_transposed", 1)
        x3T_ready = sig("x3T_ready", 1)
        logits_done = sig("logits_done", 1)
        logits_copied = sig("logits_copied", 1)
        gap_ready = sig("gap_ready", 1)
        top_exp = sig("top_exp", 1)
        chosen_ready = sig("chosen_ready", 1)
        counted = sig("counted", 1)
        meta_ready = sig("meta_ready", 1)
        x3_stored = sig("x3_stored", 16)
        meta_stored = sig("meta_stored", 16 * NT * TOPK)
        dve_b = sig("dve_b", DVE_B)

        block = ctx.enter_context(nc.Block())

        @block.sync
        def _(sp):
            for to, src in loads:
                sp.dma_start(to, src).then_inc(setup_loaded.sem, 16)

            def load_x(s):
                if later(s):
                    sp.wait_ge(z_projected.sem, z_projected.before(s))
                sp.dma_start(xT[:, :, :], ins["xT"].rearrange("(c p) t -> p c t", p=P)[:, :, bass.ds(s * T, T)]
                             ).then_inc(xT_in.sem, 16)

            def load_rows(s):
                if later(s):
                    sp.wait_ge(x1_ready.sem, x1_ready.before(s))
                sp.dma_start(x_row[:, :, :], ins["x"][bass.ds(s * T, T), :].rearrange("(t p) d -> p t d", p=P)
                             ).then_inc(x_row_in.sem, 16)
                if isinstance(s, int) and s == 0:
                    for to, src in loads_b:
                        sp.dma_start(to, src).then_inc(weights_loaded.sem, 16)

            def store_x3(s):
                sp.wait_ge(x3_ready.sem, x3_ready.at(s))
                sp.dma_start(x3_dram[bass.ds(s * T, T), :].rearrange("(t p) d -> p t d", p=P), x3[:, :, :]
                             ).then_inc(x3_stored.sem, 16)

            run_skewed(sp, nseq, {"F0": load_x, "F1": load_rows, "B6": store_x3})
            sp.wait_ge(x3_stored.sem, x3_stored.at(nseq - 1))

        @block.tensor
        def _(pe):
            mm = nc.tensor.matmul
            pe_carrier = Carrier(pe, pe_waited)

            def project(s, first, width, bank, done):
                for t in range(NT):
                    for c in range(DC):
                        last = mm(pa[:, bank + t, 0:width], xT[:, c, t * P:(t + 1) * P],
                                  w_in[:, c, first:first + width], start=c == 0, stop=c == DC - 1)
                    last.then_inc(done.sem, 1)

            def f1(s):
                if isinstance(s, int) and s == 0:
                    pe.wait_ge(setup_loaded.sem, setup_loaded.at(0))
                pe.wait_ge(xT_in.sem, xT_in.at(s))
                if later(s):
                    pe.wait_ge(x1_ready.sem, x1_ready.before(s))
                project(s, 2 * DI, REST, 0, rest_projected)

            def f2(s):
                project(s, DI, DI, 2, x_projected)

            def f3(s):
                pe.wait_ge(rest_copied.sem, rest_copied.at(s))
                project(s, 0, DI, 0, z_projected)

            def a2(s):
                pe.wait_ge(steps_ready.sem, steps_ready.at(s))
                pe.wait_ge(xs_ready.sem, xs_ready.at(s, 1))
                mm(pa[:, 2, 0:H], mat(SHIFT), q[:, 0, :], start=True, stop=False)
                mm(pa[:, 2, 0:H], mat(EDGE), q[:, 1, :], start=False, stop=True)
                mm(pa[:, 2, H:2 * H], mat(SHIFT), q[:, 1, :], start=True, stop=True)
                o = 2 * H
                mm(pa[:, 2, o:o + N // 2], mat(PREFIX), dth[:, 0, :], start=True, stop=True)
                o += N // 2
                mm(pa[:, 2, o:o + N // 2], mat(PREFIX), dth[:, 1, :], start=True, stop=False)
                mm(pa[:, 2, o:o + N // 2], mat(ONES), dth[:, 0, :], start=False, stop=True).then_inc(shifted.sem, 1)
                pe.wait_ge(zs_ready.sem, zs_ready.at(s))
                for k in range(LV):
                    mm(pa[:, k // 4, k % 4 * P:(k % 4 + 1) * P], mat(k), d_a[:, :, :].rearrange("p t h -> p (t h)"),
                       start=True, stop=True)
                mm(pa[:, 1, 3 * P:3 * P + H], mat(SUFFIX), d_a[:, 0, :], start=True, stop=True)
                mm(pa[:, 1, 3 * P + H:4 * P], mat(PREFIX), d_a[:, 1, :], start=True, stop=True
                   ).then_inc(decay_sums.sem, 1)

            def a3(s):
                pe.wait_ge(roped.sem, roped.at(s))
                pe.wait_ge(xs_ready.sem, xs_ready.at(s))
                pe_carrier.take()
                for t in range(NT):
                    for m in range(2):
                        last = nc.tensor.transpose(pa[0:N, 3, (2 * t + m) * P:(2 * t + m + 1) * P],
                                                   bcr[:, t, m, :], ident)
                last.then_inc(bc_transposed.sem, 1)
                pe.wait_ge(bcT_ready.sem, bcT_ready.at(s))
                pe.wait_ge(g_ready.sem, g_ready.at(s))
                for n, (tb, tc) in enumerate(((0, 0), (1, 1), (0, 1))):
                    last = mm(pa[:, 2, n * P:(n + 1) * P], bcT[:, tb, 0, :], bcT[:, tc, 1, :], start=True, stop=True)
                last.then_inc(cb_ready.sem, 1)

            def a4(s, k):
                if k == 0:
                    pe.wait_ge(decay_ready.sem, decay_ready.at(s))
                    pe.wait_ge(masked_ready.sem, masked_ready.at(s))
                    pe.wait_ge(cross_ready.sem, cross_ready.at(s))
                pe.wait_ge(u_ready.sem, u_ready.at(s, k + 1))
                if k >= 2:
                    pe.wait_ge(v_scaled.sem, v_scaled.at(s, k - 1))
                if k < LV:
                    for t in range(NT):
                        last = mm(pa[:, 2 * (k % 2) + t, :], masked[:, t, k, :], u[:, k % 2, t, :],
                                  start=True, stop=True)
                else:
                    last = mm(pa[:, 2 * (k % 2) + 1, :], cross[:, :], u[:, k % 2, 0, :], start=True, stop=True)
                last.then_inc(level_done.sem, 1)

            def a5(s):
                for t in range(NT):
                    pe.wait_ge(yn_ready.sem, yn_ready.at(s, t + 1))
                    for c in range(DI // P):
                        last = nc.tensor.transpose(pa[:, t, c * P:(c + 1) * P], y[:, t, c * P:(c + 1) * P], ident)
                    last.then_inc(yn_transposed.sem, 1)

            def a6(s):
                for t in range(NT):
                    pe.wait_ge(ynT_ready.sem, ynT_ready.at(s, t + 1))
                    for c in range(DI // P):
                        last = mm(pa[:, 2, t * D:(t + 1) * D], ynT[:, t, c, :], w_out[:, c, :],
                                  start=c == 0, stop=c == DI // P - 1)
                last.then_inc(out_projected.sem, 1)
                if isinstance(s, int) and s == 0:
                    pe.wait_ge(dequantised.sem, dequantised.at(0))
                    pe.wait_ge(weights_loaded.sem, weights_loaded.at(0))

            def transposes(rows, ready, done, s):
                pe.wait_ge(ready.sem, ready.at(s))
                for c in range(DC):
                    for t in range(NT):
                        last = nc.tensor.transpose(pb[:, 0, c * T + t * P:c * T + (t + 1) * P],
                                                   rows[:, t, c * P:(c + 1) * P], ident)
                last.then_inc(done.sem, 1)

            def b1(s):
                if later(s):
                    pe.wait_ge(logits_copied.sem, logits_copied.before(s))
                transposes(x1, x1_ready, x1_transposed, s)
                pe.wait_ge(x1T_ready.sem, x1T_ready.at(s))
                for j in range(FJ):
                    rows = min(P, FH - j * P)
                    if j >= 2:
                        pe.wait_ge(ffn_h.sem, ffn_h.at(s, j - 1))
                    for w, weight in enumerate((w_gate, w_up)):
                        for c in range(DC):
                            last = mm(pb[0:rows, 1 + j % 2, w * T:(w + 1) * T], weight[:, c, j * P:j * P + rows],
                                      x1T[:, c, :], start=c == 0, stop=c == DC - 1)
                    last.then_inc(ffn_projected.sem, 1)

            def b2(s):
                if later(s):
                    pe.wait_ge(meta_ready.sem, meta_ready.before(s))
                pe.wait_ge(ffn_h.sem, ffn_h.at(s))
                for t in range(NT):
                    for j in range(FJ):
                        rows = min(P, FH - j * P)
                        last = mm(pb[:, 3, t * D:(t + 1) * D], hT[0:rows, j, t * P:(t + 1) * P], w_down[0:rows, j, :],
                                  start=j == 0, stop=j == FJ - 1)
                last.then_inc(ffn_out.sem, 1)

            def b3(s):
                transposes(x2n, x2n_ready, x2_transposed, s)
                pe.wait_ge(x2T_ready.sem, x2T_ready.at(s))
                for t in range(NT):
                    for c in range(DC):
                        last = mm(pb[:, 1 + t, :], x1T[:, c, t * P:(t + 1) * P], w_qkv[:, c, 0:2 * D],
                                  start=c == 0, stop=c == DC - 1)
                    last.then_inc(qk_projected.sem, 1)
                for t in range(NT):
                    for c in range(DC):
                        last = mm(pb[:, 3, t * D:(t + 1) * D], x1T[:, c, t * P:(t + 1) * P], w_qkv[:, c, 2 * D:3 * D],
                                  start=c == 0, stop=c == DC - 1)
                last.then_inc(v_projected.sem, 1)

            def b4(s):
                pe.wait_ge(q_exp.sem, q_exp.at(s))
                for t in range(NT):
                    pe.wait_ge(wv_ready.sem, wv_ready.at(s, t + 1))
                    rhs = wv[:, t, :, :].rearrange("p a d -> p (a d)")
                    last = mm(pb[:, 1 + t, :], mat(PREFIX), rhs, start=True, stop=t == 0)
                    if t == 1:
                        last = mm(pb[:, 1 + t, :], mat(ONES), wv[:, 0, :, :].rearrange("p a d -> p (a d)"),
                                  start=False, stop=True)
                    last.then_inc(cumulated.sem, 1)

            def b5(s, j):
                if j == 0:
                    transposes(yc, yc_ready, yc_transposed, s)
                    pe.wait_ge(ycT_ready.sem, ycT_ready.at(s))
                if j >= 2:
                    pe.wait_ge(sw_h.sem, sw_h.at(s, j - 1))
                for w in range(2):
                    for c in range(DC):
                        o = (1 - w) * SH + j * P
                        last = mm(pb[:, 1 + j % 2, w * T:(w + 1) * T], w_sw[:, c, o:o + P], x1T[:, c, :],
                                  start=c == 0, stop=c == DC - 1)
                last.then_inc(sw_projected.sem, 1)

            def b6(s):
                pe.wait_ge(sw_h.sem, sw_h.at(s))
                for t in range(NT):
                    for j in range(SJ):
                        last = mm(pb[:, 3, t * D:(t + 1) * D], hT[:, j, t * P:(t + 1) * P], w_so[:, j, :],
                                  start=j == 0, stop=j == SJ - 1)
                last.then_inc(sw_out.sem, 1)

            def b7(s):
                transposes(x3, x3_ready, x3_transposed, s)
                pe.wait_ge(x3T_ready.sem, x3T_ready.at(s))
                for t in range(NT):
                    for c in range(DC):
                        last = mm(pb[:, 1, t * NE:(t + 1) * NE], x1T[:, c, t * P:(t + 1) * P], w_route[:, c, :],
                                  start=c == 0, stop=c == DC - 1)
                last.then_inc(logits_done.sem, 1)

            def b8(s):
                pe.wait_ge(chosen_ready.sem, chosen_ready.at(s))
                mm(pb[:, 3, 0:NE], mat(STRICT), chosen[:, 0, :], start=True, stop=True)
                mm(pb[:, 3, NE:2 * NE], mat(STRICT), chosen[:, 1, :], start=True, stop=False)
                mm(pb[:, 3, NE:2 * NE], mat(ONES), chosen[:, 0, :], start=False, stop=True)
                mm(pb[:, 3, 2 * NE:3 * NE], mat(ONES), chosen[:, 0, :], start=True, stop=False)
                mm(pb[:, 3, 2 * NE:3 * NE], mat(ONES), chosen[:, 1, :], start=False, stop=True
                   ).then_inc(counted.sem, 1)

            run_skewed(pe, nseq, {"F1": f1, "F2": f2, "F3": f3, "A2": a2, "A3": a3, "A4": a4, "A5": a5, "A6": a6,
                                  "B1": b1, "B2": b2, "B3": b3, "B4": b4, "B5": b5, "B6": b6, "B7": b7, "C8": b8})

        @block.scalar
        def _(act):
            act_f = nc.scalar.activation
            act.wait_ge(setup_loaded.sem, setup_loaded.at(0))
            act_f(neg_a[:, :], neg_a[:, :], ACT.Exp).then_inc(a_exp.sem, 1)

            def f1(s):
                for t in range(NT):
                    act.wait_ge(rest_projected.sem, rest_projected.at(s, t + 1))
                    act_f(rest[:, t, :], pa[:, t, 0:REST], ACT.Copy).then_inc(rest_copied.sem, 1)

            def f2(s):
                act.wait_ge(v_ready.sem, v_ready.at(s))
                act_f(eu[:, :, :], vl[:, :, :], ACT.Exp).then_inc(eu_ready.sem, 1)

            def f3(s):
                act.wait_ge(w_ready.sem, w_ready.at(s))
                act_f(lnw[:, :, :], vl[:, :, 0:H], ACT.Ln).then_inc(ln_ready.sem, 1)
                for t in range(NT):
                    act.wait_ge(x_projected.sem, x_projected.at(s, t + 1))
                    act_f(xs[:, t, :], pa[:, 2 + t, :], ACT.Silu).then_inc(xs_ready.sem, 1)
                for t in range(NT):
                    act.wait_ge(z_projected.sem, z_projected.at(s, t + 1))
                    act_f(zs[:, t, :], pa[:, t, :], ACT.Silu).then_inc(zs_ready.sem, 1)

            def a2(s):
                act.wait_ge(ang_ready.sem, ang_ready.at(s))
                act_f(cs[:, :, :, :], ang[:, :, :, :], ACT.Sin).then_inc(sin_ready.sem, 1)
                act.wait_ge(decay_sums.sem, decay_sums.at(s))
                act_f(decay[:, :, :, :].rearrange("p k t h -> p (k t h)"),
                      pa[:, 0:2, :].rearrange("p b n -> p (b n)"), ACT.Exp).then_inc(decay_ready.sem, 1)

            def a3(s):
                act.wait_ge(bc_transposed.sem, bc_transposed.at(s))
                act_f(bcT[:, :, :, :].rearrange("n t m l -> n (t m l)"), pa[0:N, 3, :], ACT.Copy
                      ).then_inc(bcT_ready.sem, 1)
                act.wait_ge(masked_ready.sem, masked_ready.at(s))
                act_f(cross[:, :], pa[:, 2, 2 * P:3 * P], ACT.Copy).then_inc(cross_ready.sem, 1)

            def a5(s):
                act.wait_ge(y_added.sem, y_added.at(s))
                for t in range(NT):
                    act_f(sq_a[:, :], y[:, t, :], ACT.Square, accum_out=yss[:, t:t + 1]).then_inc(yss_ready.sem, 1)
                    act.wait_ge(yss_ready.sem, yss_ready.at(s, t + 1))
                for t in range(NT):
                    act.wait_ge(yn_transposed.sem, yn_transposed.at(s, t + 1))
                    act_f(ynT[:, t, :, :].rearrange("p c l -> p (c l)"), pa[:, t, :], ACT.Copy
                          ).then_inc(ynT_ready.sem, 1)
                if isinstance(s, int) and s == 0:
                    act.wait_ge(weights_loaded.sem, weights_loaded.at(0))

            def transposed(done, ready, s):
                act.wait_ge(done.sem, done.at(s))
                act_f(x1T[:, :, :].rearrange("p c t -> p (c t)"), pb[:, 0, :], ACT.Copy).then_inc(ready.sem, 1)

            def b1(s):
                transposed(x1_transposed, x1T_ready, s)
                for j in range(FJ):
                    rows = min(P, FH - j * P)
                    act.wait_ge(ffn_projected.sem, ffn_projected.at(s, j + 1))
                    if j >= 2:
                        act.wait_ge(ffn_h.sem, ffn_h.at(s, j - 1))
                    act_f(sg[0:rows, j % 2, :], pb[0:rows, 1 + j % 2, 0:T], ACT.Silu,
                          scale=s_gu[0:rows, 0, j:j + 1]).then_inc(ffn_silu.sem, 1)

            def b3(s):
                for t in range(NT):
                    act.wait_ge(x2_ready.sem, x2_ready.at(s, t + 1))
                    act_f(sq_b[:, :], x2[:, t, :], ACT.Square, accum_out=rss[:, t:t + 1]).then_inc(rss_ready.sem, 1)
                    act.wait_ge(rss_ready.sem, rss_ready.at(s, t + 1))
                transposed(x2_transposed, x2T_ready, s)
                for t in range(NT):
                    act.wait_ge(qk_projected.sem, qk_projected.at(s, t + 1))
                    for m in range(2):
                        act_f(sq_b[:, :], pb[:, 1 + t, m * D:(m + 1) * D], ACT.Square,
                              accum_out=qk_ss[:, t, m:m + 1]).then_inc(qk_ss_ready.sem, 1)
                        act.wait_ge(qk_ss_ready.sem, qk_ss_ready.at(s, 2 * t + m + 1))
                act.wait_ge(qk_rms_ready.sem, qk_rms_ready.at(s))
                for t in range(NT):
                    act_f(wv[:, t, 0, :], pb[:, 1 + t, D:2 * D], ACT.Exp, scale=qk_ss[:, t, 1:2]
                          ).then_inc(k_exp.sem, 1)
                for t in range(NT):
                    act_f(eq[:, t, :], pb[:, 1 + t, 0:D], ACT.Exp, scale=qk_ss[:, t, 0:1]).then_inc(q_exp.sem, 1)

            def b5(s, j):
                if j == 0:
                    transposed(yc_transposed, ycT_ready, s)
                act.wait_ge(sw_projected.sem, sw_projected.at(s, j + 1))
                if j >= 2:
                    act.wait_ge(sw_h.sem, sw_h.at(s, j - 1))
                act_f(sg[:, j % 2, :], pb[:, 1 + j % 2, 0:T], ACT.Silu).then_inc(sw_silu.sem, 1)

            def b7(s):
                transposed(x3_transposed, x3T_ready, s)
                act.wait_ge(logits_done.sem, logits_done.at(s))
                act_f(logits[:, :, :].rearrange("p t e -> p (t e)"), pb[:, 1, 0:NT * NE], ACT.Copy
                      ).then_inc(logits_copied.sem, 1)

            def b8(s):
                act.wait_ge(gap_ready.sem, gap_ready.at(s))
                act_f(ez[:, :, :], ez[:, :, :], ACT.Exp).then_inc(top_exp.sem, 1)

            run_skewed(act, nseq, {"F1": f1, "F2": f2, "F3": f3, "A2": a2, "A3": a3, "A5": a5,
                                   "B1": b1, "B3": b3, "B5": b5, "B7": b7, "C8": b8})

        @block.gpsimd
        def _(pool):
            carrier = Carrier(pool, pool_waited)
            pa_ = Chain(pool, pool_a.sem, pool_a.per)
            pb_ = Chain(pool, pool_b.sem, pool_b.per)

            nc.gpsimd.memset(power[:, :], -0.5).then_inc(power_set.sem, 1)
            pool.wait_ge(power_set.sem, power_set.at(0))

            def exponent(ap):
                return power[:, 0:ap.shape[1]]

            def root_mean(chain, ap, n, eps):
                carrier.take()
                chain.step(nc.gpsimd.tensor_scalar(ap, ap, 1.0 / n, eps, ALU.mult, ALU.add))
                return nc.gpsimd.tensor_tensor(ap, ap, exponent(ap), ALU.pow)

            def deviation(chain, norm, mv, s):
                pool.wait_ge(norm[0].sem, norm[0].at(s))
                carrier.take()
                chain.step(nc.gpsimd.tensor_scalar(mv[:, :, 1:2], mv[:, :, 1:2], 1e-5, None, ALU.add))
                nc.gpsimd.tensor_tensor(mv[:, :, 1:2], mv[:, :, 1:2], power[:, 0:NT].unsqueeze(2), ALU.pow
                                        ).then_inc(norm[1].sem, 1)

            def f1(s):
                pa_.start(s)
                pool.wait_ge(bc_squares.sem, bc_squares.at(s))
                root_mean(pa_, ssq[:, :, :].rearrange("p t m -> p (t m)"), N, 1e-6).then_inc(bc_rms.sem, 1)

            def a5(s):
                pa_.go_on(s)
                pool.wait_ge(yss_ready.sem, yss_ready.at(s))
                root_mean(pa_, yss[:, :], DI, 1e-6).then_inc(y_rms.sem, 1)

            def a6(s):
                deviation(pa_, norm1, mv1, s)
                pa_.end()

            def b2(s):
                pb_.start(s)
                deviation(pb_, norm2, mv2, s)

            def b3(s):
                pool.wait_ge(rss_ready.sem, rss_ready.at(s))
                root_mean(pb_, rss[:, :], D, 1.1920929e-07).then_inc(x2_rms.sem, 1)
                pool.wait_ge(qk_ss_ready.sem, qk_ss_ready.at(s))
                pb_.step(root_mean(pb_, qk_ss[:, :, :].rearrange("p t m -> p (t m)"), D, 1.1920929e-07))
                carrier.take()
                nc.gpsimd.tensor_scalar(qk_ss[:, :, 0:1], qk_ss[:, :, 0:1], -1.0, None, ALU.mult
                                        ).then_inc(qk_rms_ready.sem, 1)

            def a2(s):
                pool.wait_ge(g_ready.sem, g_ready.at(s))
                pool.wait_ge(xs_ready.sem, xs_ready.at(s))
                nc.gpsimd.tensor_tensor(heads(xg[:, :, :]), heads(xs[:, :, :]), spread(g[:, :, :], 3, HD), ALU.mult
                                        ).then_inc(xg_ready.sem, 1)
                pool.wait_ge(coef_ready.sem, coef_ready.at(s))
                nc.gpsimd.tensor_tensor(heads(y[:, :, :]), heads(xs[:, :, :]), spread(coef[:, :, :], 3, HD), ALU.mult
                                        ).then_inc(y_added.sem, 1)

            def a4(s, k):
                first = 0 if k < LV else 1
                pool.wait_ge(v_scaled.sem, v_scaled.at(s, k + 1))
                pool.wait_ge(y_added.sem, y_added.at(s, k + 1))
                nc.gpsimd.tensor_tensor(y[:, first:NT, :], y[:, first:NT, :], v[:, k % 2, first:NT, :], ALU.add
                                        ).then_inc(y_added.sem, 1)

            def b6(s):
                deviation(pb_, norm3, mv2, s)
                pb_.end()

            def b8(s):
                pool.wait_ge(meta_ready.sem, meta_ready.at(s))
                carrier.take()
                for t in range(NT):
                    for j in range(TOPK):
                        nc.gpsimd.indirect_dma_start(
                            out=meta_dram, out_offset=bass.IndirectOffsetOnAxis(ap=slot[:, t, j:j + 1], axis=0),
                            in_=meta[:, t, j, :], in_offset=None).then_inc(meta_stored.sem, 16)

            run_skewed(pool, nseq, {"F1": f1, "A2": a2, "A4": a4, "A5": a5, "A6": a6, "B2L": b2, "B3": b3,
                                    "B6": b6, "C8": b8})
            pool.wait_ge(meta_stored.sem, meta_stored.at(nseq - 1))

        @block.vector
        def _(dve):
            vec = nc.vector
            carrier = Carrier(dve, dve_waited)
            ca = Chain(dve, dve_a.sem, DVE_A)
            cb_ = Chain(dve, dve_b.sem, DVE_B)

            dve.wait_ge(setup_loaded.sem, setup_loaded.at(0))
            dve.wait_ge(a_exp.sem, a_exp.at(0))
            vec.tensor_scalar(neg_a[:, :], neg_a[:, :], -1.0, None, ALU.mult)
            vec.tensor_scalar(bc_bias[:, 1, :], bc_bias[:, 1, :], float(N) ** -0.5, None, ALU.mult)
            vec.memset(base[:, :], 0.0)
            vec.memset(meta[:, :, :, :], 0)
            vec.tensor_copy(dst[:, :, :].rearrange("p t j -> p (t j)"), small[:, SM_DST:SM_TRI])
            for t in range(NT):
                last = vec.tensor_scalar(tok[:, t:t + 1], small[:, SM_P:SM_P + 1], float(t * P), None, ALU.add)
            last.then_inc(setup_done.sem, 1)
            dve.wait_ge(setup_done.sem, setup_done.at(0))

            def b_and_c():
                return rest[:, :, 0:2 * N].rearrange("p t (m n) -> p t m n", n=N)

            def f1(s):
                ca.start(s)
                dve.wait_ge(rest_copied.sem, rest_copied.at(s))
                o = 2 * N
                ca.step(vec.tensor_tensor(vl[:, :, 0:H], rest[:, :, o:o + H], spread(dt_bias[:, :], 1, NT), ALU.add))
                vec.tensor_scalar(vl[:, :, H:2 * H], rest[:, :, o + H:o + 2 * H], -1.0, None, ALU.mult)
                vec.tensor_scalar(vl[:, :, 0:H], vl[:, :, 0:H], 0.0, -9.3, ALU.min, ALU.max).then_inc(v_ready.sem, 1)
                bc = b_and_c()
                ca.step(vec.tensor_tensor(bct[:, :, :, :], bc, bc, ALU.mult))
                vec.tensor_reduce(ssq[:, :, :], bct[:, :, :, :], AX_X, ALU.add).then_inc(bc_squares.sem, 1)

            def f2(s):
                dve.wait_ge(eu_ready.sem, eu_ready.at(s))
                vec.tensor_scalar(vl[:, :, :], eu[:, :, :], 1.0, None, ALU.add).then_inc(w_ready.sem, 1)

            def f3(s):
                dve.wait_ge(bc_rms.sem, bc_rms.at(s))
                ca.step(vec.tensor_tensor(bcn[:, :, :, :], b_and_c(), spread(ssq[:, :, :], 3, N), ALU.mult))
                ca.step(vec.tensor_tensor(bcn[:, :, :, :], bcn[:, :, :, :], spread(bc_bias[:, :, :], 1, NT), ALU.mult))
                dve.wait_ge(w_ready.sem, w_ready.at(s))
                vec.tensor_scalar(rec[:, :, 0:H], vl[:, :, 0:H], -1.0, None, ALU.add)
                ca.step(vec.tensor_copy(rec[:, :, H:2 * H], vl[:, :, H:2 * H]))
                ca.step(vec.reciprocal(rec[:, :, :], rec[:, :, :]))
                ca.step(vec.tensor_tensor(dt[:, :, :], eu[:, :, 0:H], rec[:, :, 0:H], ALU.mult))
                dve.wait_ge(ln_ready.sem, ln_ready.at(s))
                ca.step(vec.tensor_tensor(dt[:, :, :], dt[:, :, :], lnw[:, :, :], ALU.mult))
                ca.step(vec.tensor_scalar(dt[:, :, :], dt[:, :, :], DT_MIN, DT_MAX, ALU.max, ALU.min))
                vec.tensor_tensor(d_a[:, :, :], dt[:, :, :], spread(neg_a[:, :], 1, NT), ALU.mult)
                vec.tensor_tensor(ld[:, :, :], dt[:, :, :], rec[:, :, H:2 * H], ALU.mult)
                ca.step(vec.tensor_reduce(dtm[:, :], dt[:, :, :], AX_X, ALU.add))
                vec.tensor_tensor(q[:, :, :], dt[:, :, :], ld[:, :, :], ALU.subtract)
                for t in range(NT):
                    last = vec.tensor_scalar(dth[:, t, :], rest[:, t, REST - N // 2:REST], dtm[:, t:t + 1], 1.0 / H,
                                             ALU.mult, ALU.mult)
                last.then_inc(steps_ready.sem, 1)

            def a2(s):
                ca.go_on(s)
                dve.wait_ge(shifted.sem, shifted.at(s))
                cum = pa[:, 2, 2 * H:2 * H + N].rearrange("p (t n) -> p t n", t=NT)
                vec.tensor_scalar(ang[:, :, 0, :], cum, float(np.pi / 2), None, ALU.add)
                ca.step(vec.tensor_copy(ang[:, :, 1, :], cum))
                ca.step(vec.tensor_scalar(turns[:, :, :, :], ang[:, :, :, :], float(0.5 / np.pi), MAGIC,
                                          ALU.mult, ALU.add))
                ca.step(vec.tensor_scalar(turns[:, :, :, :], turns[:, :, :, :], MAGIC, None, ALU.subtract))
                flat = "p t c n -> p (t c n)"
                an, tu = ang[:, :, :, :].rearrange(flat), turns[:, :, :, :].rearrange(flat)
                ca.step(vec.scalar_tensor_tensor(an, tu, -TWO_PI_HI, an, ALU.mult, ALU.add))
                ca.step(vec.scalar_tensor_tensor(an, tu, -TWO_PI_LO, an, ALU.mult, ALU.add))
                vec.tensor_scalar(an, an, 3.1415925, -3.1415925, ALU.min, ALU.max).then_inc(ang_ready.sem, 1)
                vec.tensor_tensor(g[:, :, :], ld[:, :, :], pa[:, 2, 0:2 * H].rearrange("p (t h) -> p t h", t=NT),
                                  ALU.add).then_inc(g_ready.sem, 1)
                dve.wait_ge(sin_ready.sem, sin_ready.at(s))
                half = N // 2

                def halves(ap):
                    return ap.rearrange("p t m (f n) -> p t (m f) n", n=half)

                vec.tensor_tensor(halves(bct[:, :, :, :]), halves(bcn[:, :, :, :]), spread(cs[:, :, 0, :], 2, 4), ALU.mult)
                ca.step(vec.tensor_tensor(halves(bcu[:, :, :, :]), halves(bcn[:, :, :, :]), spread(cs[:, :, 1, :], 2, 4),
                                          ALU.mult))
                vec.tensor_tensor(bcr[:, :, :, 0:half], bct[:, :, :, 0:half], bcu[:, :, :, half:N], ALU.add)
                vec.tensor_tensor(bcr[:, :, :, half:N], bct[:, :, :, half:N], bcu[:, :, :, 0:half], ALU.subtract
                                  ).then_inc(roped.sem, 1)
                dve.wait_ge(roped.sem, roped.at(s))
                ca.step(vec.tensor_tensor(bct[:, :, 0, :], bcr[:, :, 0, :], bcr[:, :, 1, :], ALU.mult))
                ca.step(vec.tensor_reduce(cb[:, :], bct[:, :, 0, :], AX_X, ALU.add))
                vec.tensor_tensor(coef[:, :, :], ld[:, :, :], spread(cb[:, :], 2, H), ALU.mult
                                  ).then_inc(coef_ready.sem, 1)

            def a3(s):
                dve.wait_ge(cb_ready.sem, cb_ready.at(s))
                for t in range(NT):
                    vec.tensor_tensor(masked[:, t, :, :], spread(pa[:, 2, t * P:(t + 1) * P], 1, LV),
                                      const[:, MASK0:MASK0 + LV, :], ALU.mult).then_inc(masked_ready.sem, 1)
                dve.wait_ge(decay_ready.sem, decay_ready.at(s))
                dve.wait_ge(xg_ready.sem, xg_ready.at(s))
                decayed(s, 0)
                decayed(s, 1)

            def decayed(s, k):
                tiles = NT if k < LV else 1
                if k >= 2:
                    dve.wait_ge(level_done.sem, level_done.at(s, k - 1))
                vec.tensor_tensor(heads(u[:, k % 2, 0:tiles, :]), heads(xg[:, 0:tiles, :]),
                                  spread(decay[:, k, 0:tiles, :], 3, HD), ALU.mult).then_inc(u_ready.sem, 1)

            def a4(s, k):
                first = 0 if k < LV else 1
                dve.wait_ge(level_done.sem, level_done.at(s, k + 1))
                if k >= 2:
                    dve.wait_ge(y_added.sem, y_added.at(s, k))
                b = 2 * (k % 2)
                vec.tensor_tensor(heads(v[:, k % 2, first:NT, :]), heads(pa[:, b + first:b + NT, :]),
                                  spread(decay[:, k, first:NT, :], 3, HD), ALU.mult).then_inc(v_scaled.sem, 1)
                if k + 2 <= LV:
                    decayed(s, k + 2)

            def a5(s):
                ca.go_on(s)
                dve.wait_ge(y_rms.sem, y_rms.at(s))
                for t in range(NT):
                    vec.scalar_tensor_tensor(y[:, t, :], y[:, t, :], yss[:, t:t + 1], zs[:, t, :], ALU.mult, ALU.mult
                                             ).then_inc(yn_ready.sem, 1)

            def a6(s):
                ca.go_on(s)
                dve.wait_ge(out_projected.sem, out_projected.at(s))
                dve.wait_ge(x_row_in.sem, x_row_in.at(s))
                ca.step(vec.tensor_tensor(r1[:, :, :], x_row[:, :, :], pa[:, 2, :].rearrange("p (t d) -> p t d", t=NT),
                                          ALU.add))
                if later(s):
                    dve.wait_ge(x2_ready.sem, x2_ready.before(s))
                layer_norm(ca, s, r1, st1, mv1, norm1, x1, x1_ready)
                ca.end()
                if isinstance(s, int) and s == 0:
                    dve.wait_ge(weights_loaded.sem, weights_loaded.at(0))
                    for w in (w_gate, w_up):
                        vec.tensor_scalar(w[:, :, :], w[:, :, :].bitcast(I32), -128.0, None, ALU.add
                                          ).then_inc(dequantised.sem, 1)
                    vec.tensor_scalar(w_down[:, 0:FJ - 1, :], w_down[:, 0:FJ - 1, :].bitcast(I32), -128.0, None, ALU.add
                                      ).then_inc(dequantised.sem, 1)
                    r = FH - (FJ - 1) * P
                    vec.tensor_scalar(w_down[0:r, FJ - 1, :], w_down[0:r, FJ - 1, :].bitcast(I32), -128.0, None, ALU.add
                                      ).then_inc(dequantised.sem, 1)

            def layer_norm(chain, s, src, stats, mv, norm, to, done):
                for t in range(NT):
                    last = vec.bn_stats(stats[:, t, :], src[:, t, :])
                chain.step(last)
                carrier.take()
                for t in range(NT):
                    last = vec.bn_aggr(mv[:, t, :], stats[:, t, :])
                last.then_inc(norm[0].sem, 1)
                dve.wait_ge(norm[1].sem, norm[1].at(s))
                for t in range(NT):
                    vec.tensor_scalar(to[:, t, :], src[:, t, :], mv[:, t, 0:1], mv[:, t, 1:2], ALU.subtract, ALU.mult
                                      ).then_inc(done.sem, 1)

            def b1(s):
                for j in range(FJ):
                    rows = min(P, FH - j * P)
                    dve.wait_ge(ffn_silu.sem, ffn_silu.at(s, j + 1))
                    vec.scalar_tensor_tensor(hT[0:rows, j, :], pb[0:rows, 1 + j % 2, T:2 * T], s_gu[0:rows, 1, j:j + 1],
                                             sg[0:rows, j % 2, :], ALU.mult, ALU.mult).then_inc(ffn_h.sem, 1)

            def b2(s):
                cb_.start(s)
                dve.wait_ge(ffn_out.sem, ffn_out.at(s))
                dve.wait_ge(x1_ready.sem, x1_ready.at(s))
                cb_.step(vec.tensor_tensor(r2[:, :, :], pb[:, 3, :].rearrange("p (t d) -> p t d", t=NT),
                                           spread(s_down[:, :], 1, NT), ALU.mult))
                cb_.step(vec.tensor_tensor(r2[:, :, :], r2[:, :, :], x1[:, :, :], ALU.add))
                layer_norm(cb_, s, r2, st2, mv2, norm2, x2, x2_ready)

            def b3(s):
                dve.wait_ge(x2_rms.sem, x2_rms.at(s))
                for t in range(NT):
                    vec.tensor_scalar(x2n[:, t, :], x2[:, t, :], rss[:, t:t + 1], None, ALU.mult
                                      ).then_inc(x2n_ready.sem, 1)
                dve.wait_ge(v_projected.sem, v_projected.at(s))
                for t in range(NT):
                    dve.wait_ge(k_exp.sem, k_exp.at(s, t + 1))
                    vec.tensor_tensor(wv[:, t, 1, :], wv[:, t, 0, :], pb[:, 3, t * D:(t + 1) * D], ALU.mult
                                      ).then_inc(wv_ready.sem, 1)

            def b4(s):
                dve.wait_ge(q_exp.sem, q_exp.at(s))
                cb_.step(vec.tensor_scalar(eq[:, :, :], eq[:, :, :], 1.0, None, ALU.add))
                dve.wait_ge(cumulated.sem, cumulated.at(s))
                cb_.step(vec.scalar_tensor_tensor(den[:, :, :], pb[:, 1:1 + NT, 0:D], 1e-6, eq[:, :, :],
                                                  ALU.add, ALU.mult))
                cb_.step(vec.reciprocal(den[:, :, :], den[:, :, :]))
                vec.tensor_tensor(yc[:, :, :], den[:, :, :], pb[:, 1:1 + NT, D:2 * D], ALU.mult
                                  ).then_inc(yc_ready.sem, 1)

            def b5(s, j):
                dve.wait_ge(sw_silu.sem, sw_silu.at(s, j + 1))
                vec.tensor_tensor(hT[:, j, :], pb[:, 1 + j % 2, T:2 * T], sg[:, j % 2, :], ALU.mult
                                  ).then_inc(sw_h.sem, 1)

            def b6(s):
                dve.wait_ge(sw_out.sem, sw_out.at(s))
                cb_.step(vec.scalar_tensor_tensor(r2[:, :, :], x2[:, :, :], 2.0,
                                                  pb[:, 3, :].rearrange("p (t d) -> p t d", t=NT), ALU.mult, ALU.add))
                if later(s):
                    dve.wait_ge(x3_stored.sem, x3_stored.before(s))
                layer_norm(cb_, s, r2, st2, mv2, norm3, x3, x3_ready)

            def b7(s):
                dve.wait_ge(logits_copied.sem, logits_copied.at(s))
                carrier.take()
                for t in range(NT):
                    last = vec.max(top[:, t, :], logits[:, t, :])
                cb_.step(last)
                if later(s):
                    dve.wait_ge(meta_stored.sem, meta_stored.before(s))
                carrier.take()
                for t in range(NT):
                    vec.max_index(topi[:, t, :], top[:, t, :], logits[:, t, :])
                vec.tensor_tensor(ez[:, :, :], top[:, :, 0:TOPK], top[:, :, 0:1].broadcast_to([P, NT, TOPK]),
                                  ALU.subtract).then_inc(gap_ready.sem, 1)
                dve.wait_ge(gap_ready.sem, gap_ready.at(s))
                cb_.step(vec.tensor_copy(topf[:, :, :], topi[:, :, 0:TOPK]))
                for t in range(NT):
                    last = vec.tensor_tensor(hot[:, t, :, :], spread(small[:, SM_E:SM_DST], 1, TOPK),
                                             spread(topf[:, t, :], 2, NE), ALU.is_equal)
                cb_.step(last)
                vec.tensor_reduce(chosen[:, :, :], hot[:, :, :, :].rearrange("p t j e -> p t e j"), AX_X, ALU.add
                                  ).then_inc(chosen_ready.sem, 1)

            def b8(s):
                cb_.go_on(s)
                dve.wait_ge(top_exp.sem, top_exp.at(s))
                cb_.step(vec.tensor_reduce(esum[:, :], ez[:, :, :], AX_X, ALU.add))
                cb_.step(vec.reciprocal(esum[:, :], esum[:, :]))
                vec.tensor_tensor(meta[:, :, :, 2].bitcast(F32), ez[:, :, :], spread(esum[:, :], 2, TOPK), ALU.mult)
                vec.tensor_copy(meta[:, :, :, 0], dst[:, :, :])
                cb_.step(vec.tensor_copy(meta[:, :, :, 1], spread(tok[:, :], 2, TOPK)))
                vec.tensor_scalar(dst[:, :, :], dst[:, :, :], float(T * TOPK), None, ALU.add)
                vec.tensor_scalar(tok[:, :], tok[:, :], float(T), None, ALU.add)
                dve.wait_ge(counted.sem, counted.at(s))
                cb_.step(vec.tensor_tensor(pos[:, :, :], pb[:, 3, 0:NT * NE].rearrange("p (t e) -> p t e", t=NT),
                                           spread(base[:, :], 1, NT), ALU.add))
                vec.tensor_tensor(base[:, :], base[:, :], pb[:, 3, NT * NE:(NT + 1) * NE], ALU.add)
                for t in range(NT):
                    last = vec.tensor_tensor(hot_pos[:, t, :, :], hot[:, t, :, :], spread(pos[:, t, :], 1, TOPK), ALU.mult)
                cb_.step(last)
                cb_.step(vec.tensor_reduce(slot_f[:, :, :], hot_pos[:, :, :, :], AX_X, ALU.add))
                flat = "p t j -> p (t j)"
                vec.scalar_tensor_tensor(slot[:, :, :].rearrange(flat), topf[:, :, :].rearrange(flat), float(cap),
                                         slot_f[:, :, :].rearrange(flat), ALU.mult, ALU.add
                                         ).then_inc(meta_ready.sem, 1)
                cb_.end()

            run_skewed(dve, nseq, {"F1": f1, "F2": f2, "F3": f3, "A2": a2, "A3": a3, "A4": a4, "A5": a5, "A6": a6,
                                   "B1": b1, "B2L": b2, "B3": b3, "B4": b4, "B5": b5, "B6": b6, "B7": b7, "C8": b8})


def heads(ap):
    return ap.rearrange("p t (h d) -> p t h d", d=HD)


def experts_block(nc, ins, ntok, cap, ntile, ident, small, base, meta_dram, x3_dram, yk_dram):
    pieces = 3
    XS = UN // 2
    with ExitStack() as ctx:
        def sb(name, shape, dt=F32):
            return ctx.enter_context(nc.sbuf_tensor(name, shape, dt))

        def sig(name, per):
            return Signal(ctx.enter_context(nc.semaphore(name)), per)

        w_ug = sb("w_ug", [P, NE, 2, DC, 2 * EH], BF16)
        w_dn = sb("w_dn", [EC, NE, 2, EJ, D], BF16)
        stage = sb("stage", [P, 2, EJ * D])
        count = sb("count", [P, NE + 1])
        tiles_of = sb("tiles_of", [P, NE])
        upto = sb("upto", [P, NE])
        tri = sb("tri", [P, NE, NE])
        pad_slot = sb("pad_slot", [P, NE + 1], U32)
        pad_meta = sb("pad_meta", [P, 4], U32)
        tile_e = sb("tile_e", [1, ntile])
        tile_o = sb("tile_o", [1, ntile])
        table = sb("table", [1, 2, ntile], I32)
        meta = sb("meta_in", [P, UN, 4], U32)
        xin = sb("xin", [P, XS, D])
        xh = sb("xh", [P, 2, 2, DC, P], BF16)
        gate_hid = sb("gate_hid", [P, 3, EH])
        gate, hid = gate_hid[:, 0, :], gate_hid[:, 1:3, :]
        passed = gate_hid[0:1, :, :].rearrange("p a b -> p (a b)").bitcast(BF16)[:, 0:ntile * NE].rearrange(
            "p (i e) -> p i e", e=NE)
        hh = sb("hh", [EC, 2, 2, EJ, P], BF16)
        yo = sb("yo", [P, 2, D])

        pu = ctx.enter_context(nc.psum_tensor("pu", [P, 4, 512], F32))
        ph = ctx.enter_context(nc.psum_tensor("ph", [P, 2, 512], F32))
        px = ctx.enter_context(nc.psum_tensor("px", [P, 512], F32))
        py = ctx.enter_context(nc.psum_tensor("py", [P, 512], F32))
        ident = ident[:, :]

        piece_in = [sig(f"piece_in{n}", 16) for n in range(2)]
        high_done = sig("high_done", pieces)
        weights_ready = sig("weights_ready", pieces)
        list_step = sig("list_step", 14)
        pads_ready = sig("pads_ready", 1)
        pads_stored = sig("pads_stored", 16 * (NE + 1))
        table_ready = sig("table_ready", 1)
        pool_waited, sp_waited = (ctx.enter_context(nc.semaphore(f"{n}_waited_e")) for n in ("pool", "sp"))
        meta_in = [sig(f"meta_in{n}", 16) for n in range(UN)]
        x_in = [sig(f"x_in{n}", 16) for n in range(XS)]
        x_transposed = sig("x_transposed", 1)
        x_high = sig("x_high", 1)
        x_split = sig("x_split", 1)
        ug_done = sig("ug_done", 1)
        gate_ready = sig("gate_ready", 1)
        hid_ready = sig("hid_ready", 1)
        h_transposed = sig("h_transposed", 1)
        h_high = sig("h_high", 1)
        h_split = sig("h_split", 1)
        down_done = sig("down_done", 1)
        y_ready = sig("y_ready", 1)
        y_stored = [sig(f"y_stored{n}", 16) for n in range(2)]

        def piece_views(e, k):
            if k < DC:
                return P, 2 * EH, lambda part: w_ug[:, e, part, k, :]
            return EC, EJ * D, lambda part: w_dn[:, e, part, :, :].rearrange("p j d -> p (j d)")

        def steps(eng, run, first, last):
            lo, hi = NE // UN, ntile // UN - 1
            for i in range(first, UN * lo):
                run(i // UN, i % UN)
            if hi > lo:
                with eng.Fori(lo, hi) as r:
                    for m in range(UN):
                        run(r, m)
            for i in range(UN * max(hi, lo), last):
                run(i // UN, i % UN)

        def parts(r, m, shift, **runs):
            r, m = r + (m + shift) // UN, (m + shift) % UN
            if not isinstance(r, int) or 0 <= UN * r + m < ntile:
                for run in runs.values():
                    run(r, m)

        def pieces_of(r, m, run, ahead=0):
            if isinstance(r, int):
                for n in range(pieces * (UN * r + m + 1) + ahead, pieces * (UN * r + m + 2) + ahead):
                    if n < NE * pieces:
                        run(n // pieces, n % pieces)

        block = ctx.enter_context(nc.Block())

        @block.sync
        def _(sp):
            def load_piece(e, k):
                n = e * pieces + k
                rows, width, _ = piece_views(e, k)
                if n >= 2:
                    sp.wait_ge(weights_ready.sem, n - 1)
                src = ins["w_ug"][e, k * P:(k + 1) * P, :] if k < DC else \
                    ins["w_dn"][e].rearrange("(j p) d -> p j d", p=EC)
                to = stage[0:rows, n % 2, 0:width]
                if k == DC:
                    to = to.rearrange("p (j d) -> p j d", j=EJ)
                sp.dma_start(to, src).then_inc(piece_in[n % 2].sem, 16)

            carrier = Carrier(sp, sp_waited)

            def load_meta(r, m):
                i = UN * r + m
                if later(i, UN):
                    sp.wait_ge(y_stored[m % 2].sem, y_stored[m % 2].at(UN // 2 * (r - 1) + m // 2))
                carrier.take()
                row = sp.value_load(table[0:1, 1, bass.ds(i, 1)], min_val=0, max_val=NE * cap)
                sp.dma_start(meta[:, m, :], meta_dram[bass.ds(row, P), :]).then_inc(meta_in[m].sem, 16)

            load_piece(0, 0)
            load_piece(0, 1)
            sp.wait_ge(pads_stored.sem, pads_stored.at(0))
            sp.wait_ge(table_ready.sem, table_ready.at(0))
            for i in range(3):
                load_meta(0, i)

            def step(r, m):
                parts(r, m, 4, run=load_meta)
                pieces_of(r, m, load_piece, 2)

            steps(sp, step, -1, ntile)

        @block.tensor
        def _(pe):
            mm = nc.tensor.matmul

            def transpose_x(r, m):
                i = UN * r + m
                pe.wait_ge(x_in[m % XS].sem, x_in[m % XS].at(2 * r + m // XS))
                if later(i):
                    pe.wait_ge(x_split.sem, x_split.before(i))
                for c in range(DC):
                    last = nc.tensor.transpose(px[:, c * P:(c + 1) * P], xin[:, m % XS, c * P:(c + 1) * P], ident)
                last.then_inc(x_transposed.sem, 1)

            def up_gate(r, m):
                i = UN * r + m
                b = m % 2
                e = pe.value_load(table[0:1, 0, bass.ds(i, 1)], min_val=0, max_val=NE - 1)
                pe.wait_ge(x_split.sem, x_split.at(i))
                pe.wait_ge(weights_ready.sem, (e + 1) * pieces)
                if later(i, 2):
                    pe.wait_ge(hid_ready.sem, hid_ready.at(i - 2))
                for w in range(2):
                    n = 0
                    for c in range(DC):
                        for xp, wp in ((0, 0), (0, 1), (1, 0)):
                            last = mm(pu[:, 2 * b + w, 0:EH], xh[:, b, xp, c, :],
                                      w_ug[:, bass.ds(e, 1), wp, c, w * EH:(w + 1) * EH],
                                      start=n == 0, stop=n == 3 * DC - 1)
                            n += 1
                last.then_inc(ug_done.sem, 1)

            def transpose_h(r, m):
                i = UN * r + m
                b = m % 2
                pe.wait_ge(hid_ready.sem, hid_ready.at(i))
                if later(i, 2):
                    pe.wait_ge(h_split.sem, h_split.at(i - 2))
                for j in range(EJ):
                    last = nc.tensor.transpose(ph[0:EC, b, j * P:(j + 1) * P], hid[:, b, j * EC:(j + 1) * EC], ident)
                last.then_inc(h_transposed.sem, 1)

            def down(r, m):
                i = UN * r + m
                b = m % 2
                e = pe.value_load(table[0:1, 0, bass.ds(i, 1)], min_val=0, max_val=NE - 1)
                pe.wait_ge(h_split.sem, h_split.at(i))
                if later(i):
                    pe.wait_ge(y_ready.sem, y_ready.before(i))
                n = 0
                for j in range(EJ):
                    for hp, wp in ((0, 0), (0, 1), (1, 0)):
                        last = mm(py[:, 0:D], hh[:, b, hp, j, :], w_dn[:, bass.ds(e, 1), wp, j, :],
                                  start=n == 0, stop=n == 3 * EJ - 1)
                        n += 1
                last.then_inc(down_done.sem, 1)

            pe.wait_ge(table_ready.sem, table_ready.at(0))

            def step(r, m):
                parts(r, m, 0, run=up_gate)
                parts(r, m, -1, run=transpose_h)
                parts(r, m, 1, run=transpose_x)
                parts(r, m, -2, run=down)

            steps(pe, step, -1, ntile + 2)

        @block.scalar
        def _(act):
            act_f = nc.scalar.activation

            def high(e, k):
                n = e * pieces + k
                rows, width, part = piece_views(e, k)
                act.wait_ge(piece_in[n % 2].sem, 16 * (n // 2 + 1))
                act_f(part(0), stage[0:rows, n % 2, 0:width], ACT.Copy).then_inc(high_done.sem, 1)

            def x_part(r, m):
                i = UN * r + m
                act.wait_ge(x_transposed.sem, x_transposed.at(i))
                if later(i, 2):
                    act.wait_ge(ug_done.sem, ug_done.at(i - 2))
                act_f(xh[:, m % 2, 0, :, :].rearrange("p c l -> p (c l)"), px[:, 0:D], ACT.Copy
                      ).then_inc(x_high.sem, 1)

            def gate_part(r, m):
                i = UN * r + m
                act.wait_ge(ug_done.sem, ug_done.at(i))
                if later(i):
                    act.wait_ge(hid_ready.sem, hid_ready.before(i))
                act_f(gate, pu[:, 2 * (m % 2) + 1, 0:EH], ACT.Silu).then_inc(gate_ready.sem, 1)

            def h_part(r, m):
                i = UN * r + m
                act.wait_ge(h_transposed.sem, h_transposed.at(i))
                if later(i, 2):
                    act.wait_ge(down_done.sem, down_done.at(i - 2))
                act_f(hh[:, m % 2, 0, :, :].rearrange("p j l -> p (j l)"), ph[0:EC, m % 2, :], ACT.Copy
                      ).then_inc(h_high.sem, 1)

            def step(r, m):
                pieces_of(r, m, high)
                parts(r, m, -1, run=h_part)
                parts(r, m, 1, run=x_part)
                parts(r, m, 0, run=gate_part)

            steps(act, step, -1, ntile + 2)

        @block.vector
        def _(dve):
            vec = nc.vector
            chain = Chain(dve, list_step.sem, list_step.per)
            vec.memset(count[:, NE:NE + 1], 0.0)
            vec.memset(pad_meta[:, 1:4], 0)
            vec.memset(pad_meta[:, 0:1], 2 ** 30)
            chain.step(vec.tensor_copy(count[:, 0:NE], base[:, :]))
            vec.tensor_scalar(pad_slot[:, :].bitcast(F32), count[:, :], small[:, SM_P:SM_P + 1], None, ALU.add)
            chain.step(vec.tensor_scalar(tiles_of[:, :], count[:, 0:NE], 1.0 / P, (P - 1) / P - 0.5 + 0.5 / P,
                                         ALU.mult, ALU.add))
            vec.scalar_tensor_tensor(count[:, 0:NE], small[:, SM_E:SM_DST], float(cap),
                                     pad_slot[:, 0:NE].bitcast(F32), ALU.mult, ALU.add)
            chain.step(vec.tensor_scalar(count[:, NE:NE + 1], pad_slot[:, NE:NE + 1].bitcast(F32), float(NE * cap), None,
                                         ALU.add))
            vec.tensor_copy(pad_slot[:, :], count[:, :]).then_inc(pads_ready.sem, 1)
            chain.step(vec.tensor_scalar(tiles_of[:, :], tiles_of[:, :], MAGIC, None, ALU.add))
            chain.step(vec.tensor_scalar(tiles_of[:, :], tiles_of[:, :], MAGIC, 1.0, ALU.subtract, ALU.max))
            chain.step(vec.tensor_tensor(tri[:, :, :], small[:, SM_TRI:SM_I].rearrange("p (a b) -> p a b", a=NE),
                                         spread(tiles_of[:, :], 1, NE), ALU.mult))
            chain.step(vec.tensor_reduce(upto[:, :], tri[:, :, :], AX_X, ALU.add))
            number = small[0:1, SM_I:SM_I + ntile]
            chain.step(vec.tensor_tensor(passed[:, :, :], spread(upto[0:1, :], 1, ntile), spread(number, 2, NE), ALU.is_le))
            chain.step(vec.tensor_reduce(tile_e[:, :], passed[:, :, :], AX_X, ALU.add))
            chain.step(vec.tensor_tensor(passed[:, :, :], passed[:, :, :], spread(tiles_of[0:1, :], 1, ntile), ALU.mult))
            chain.step(vec.tensor_reduce(tile_o[:, :], passed[:, :, :], AX_X, ALU.add))
            chain.step(vec.tensor_tensor(tile_o[:, :], number, tile_o[:, :], ALU.subtract))
            chain.step(vec.tensor_scalar(tile_o[:, :], tile_o[:, :], float(P), None, ALU.mult))
            chain.step(vec.scalar_tensor_tensor(tile_o[:, :], tile_e[:, :], float(cap), tile_o[:, :], ALU.mult, ALU.add))
            chain.end()
            vec.tensor_scalar(table[:, 0, :], tile_e[:, :], float(NE - 1), None, ALU.min)
            vec.tensor_scalar(table[:, 1, :], tile_o[:, :], float(NE * cap), None, ALU.min).then_inc(table_ready.sem, 1)

            def low(e, k):
                n = e * pieces + k
                rows, width, part = piece_views(e, k)
                dve.wait_ge(high_done.sem, n + 1)
                vec.tensor_tensor(part(1), stage[0:rows, n % 2, 0:width], part(0), ALU.subtract
                                  ).then_inc(weights_ready.sem, 1)

            def x_part(r, m):
                i = UN * r + m
                dve.wait_ge(x_high.sem, x_high.at(i))
                vec.tensor_tensor(xh[:, m % 2, 1, :, :].rearrange("p c l -> p (c l)"), px[:, 0:D],
                                  xh[:, m % 2, 0, :, :].rearrange("p c l -> p (c l)"), ALU.subtract
                                  ).then_inc(x_split.sem, 1)

            def hidden(r, m):
                i = UN * r + m
                dve.wait_ge(gate_ready.sem, gate_ready.at(i))
                if later(i, 2):
                    dve.wait_ge(h_transposed.sem, h_transposed.at(i - 2))
                vec.tensor_tensor(hid[:, m % 2, :], pu[:, 2 * (m % 2), 0:EH], gate, ALU.mult
                                  ).then_inc(hid_ready.sem, 1)

            def h_part(r, m):
                i = UN * r + m
                dve.wait_ge(h_high.sem, h_high.at(i))
                vec.tensor_tensor(hh[:, m % 2, 1, :, :].rearrange("p j l -> p (j l)"), ph[0:EC, m % 2, :],
                                  hh[:, m % 2, 0, :, :].rearrange("p j l -> p (j l)"), ALU.subtract
                                  ).then_inc(h_split.sem, 1)

            def y_part(r, m):
                i = UN * r + m
                dve.wait_ge(down_done.sem, down_done.at(i))
                if later(i, 2):
                    dve.wait_ge(y_stored[m % 2].sem, y_stored[m % 2].at(UN // 2 * r + m // 2 - 1))
                vec.tensor_scalar(yo[:, m % 2, :], py[:, 0:D], meta[:, m, 2:3].bitcast(F32), None, ALU.mult
                                  ).then_inc(y_ready.sem, 1)

            def step(r, m):
                pieces_of(r, m, low)
                parts(r, m, -1, run=h_part)
                parts(r, m, 1, run=x_part)
                parts(r, m, 0, run=hidden)
                parts(r, m, -2, run=y_part)

            steps(dve, step, -1, ntile + 2)

        @block.gpsimd
        def _(pool):
            carrier = Carrier(pool, pool_waited)
            pool.wait_ge(pads_ready.sem, pads_ready.at(0))
            for e in range(NE + 1):
                nc.gpsimd.indirect_dma_start(
                    out=meta_dram, out_offset=bass.IndirectOffsetOnAxis(ap=pad_slot[:, e:e + 1], axis=0),
                    in_=pad_meta[:, :], in_offset=None).then_inc(pads_stored.sem, 16)
            def gather(r, m):
                i = UN * r + m
                pool.wait_ge(meta_in[m].sem, meta_in[m].at(r))
                if later(i, XS):
                    pool.wait_ge(x_transposed.sem, x_transposed.at(i - XS))
                carrier.take()
                nc.gpsimd.indirect_dma_start(
                    out=xin[:, m % XS, :], out_offset=None, in_=x3_dram,
                    in_offset=bass.IndirectOffsetOnAxis(ap=meta[:, m, 1:2], axis=0)
                ).then_inc(x_in[m % XS].sem, 16)

            def scatter(r, m):
                i = UN * r + m
                pool.wait_ge(y_ready.sem, y_ready.at(i))
                carrier.take()
                nc.gpsimd.indirect_dma_start(
                    out=yk_dram, out_offset=bass.IndirectOffsetOnAxis(ap=meta[:, m, 0:1], axis=0),
                    in_=yo[:, m % 2, :], in_offset=None, bounds_check=ntok * TOPK - 1, oob_is_err=False
                ).then_inc(y_stored[m % 2].sem, 16)

            def step(r, m):
                parts(r, m, -3, run=scatter)
                parts(r, m, 3, run=gather)

            gather(0, 0)
            gather(0, 1)
            steps(pool, step, -1, ntile + 3)
            for n in range(2):
                pool.wait_ge(y_stored[n].sem, y_stored[n].at(ntile // 2 - 1))


def combine_block(nc, nseq, x3_dram, yk_dram, out):
    with ExitStack() as ctx:
        def sb(name, shape, dt=F32):
            return ctx.enter_context(nc.sbuf_tensor(name, shape, dt))

        def sig(name, per):
            return Signal(ctx.enter_context(nc.semaphore(name)), per)

        rows = sb("rows", [P, 2, NT, TOPK * D])
        res = sb("res", [P, 2, NT, D])
        st = sb("st", [P, NT, 6])
        mv = sb("mv", [P, NT, 2])
        fin = sb("fin", [P, 2, NT, D])
        loaded = [sig(f"loaded{n}", 32) for n in range(2)]
        halved = sig("halved", 1)
        summed = sig("summed", 1)
        norm_step = sig("norm_step", 2)
        power = sb("power_c", [P, 1])
        pool_waited, dve_waited = (ctx.enter_context(nc.semaphore(f"{n}_waited_c")) for n in ("pool", "dve"))
        power_set = sig("power_set", 1)
        shifted = sig("shifted_c", 1)
        variance_ready = sig("variance_ready", 1)
        deviation_ready = sig("deviation_ready", 1)
        normed = sig("normed", 1)
        stored = [sig(f"stored{n}", 16) for n in range(2)]
        block = ctx.enter_context(nc.Block())

        def pairs(eng, run):
            for m in range(min(2, nseq)):
                run(m, m, 0)
            if nseq > 2:
                with eng.Fori(1, nseq // 2) as r:
                    for m in range(2):
                        run(2 * r + m, m, r)

        @block.sync
        def _(sp):
            def load(i, m, r):
                if later(i, 2):
                    sp.wait_ge(normed.sem, normed.at(i - 2))
                sp.dma_start(rows[:, m, :, :], yk_dram.rearrange("(n k) d -> n (k d)", k=TOPK)[bass.ds(i * T, T), :]
                             .rearrange("(t p) d -> p t d", p=P)).then_inc(loaded[m].sem, 16)
                sp.dma_start(res[:, m, :, :], x3_dram[bass.ds(i * T, T), :].rearrange("(t p) d -> p t d", p=P)
                             ).then_inc(loaded[m].sem, 16)

            pairs(sp, load)

        @block.gpsimd
        def _(pool):
            carrier = Carrier(pool, pool_waited)
            nc.gpsimd.memset(power[:, :], -0.5).then_inc(power_set.sem, 1)
            pool.wait_ge(power_set.sem, power_set.at(0))

            def halve(i, m, r):
                pool.wait_ge(loaded[m].sem, loaded[m].at(r))
                nc.gpsimd.tensor_tensor(rows[:, m, :, 0:2 * D], rows[:, m, :, 0:2 * D], rows[:, m, :, 2 * D:4 * D],
                                        ALU.add).then_inc(halved.sem, 1)
                pool.wait_ge(variance_ready.sem, variance_ready.at(i))
                carrier.take()
                nc.gpsimd.tensor_scalar(mv[:, :, 1:2], mv[:, :, 1:2], 1e-5, None, ALU.add).then_inc(shifted.sem, 1)
                pool.wait_ge(shifted.sem, shifted.at(i))
                nc.gpsimd.tensor_tensor(mv[:, :, 1:2], mv[:, :, 1:2], spread(power[:, :], 1, NT), ALU.pow
                                        ).then_inc(deviation_ready.sem, 1)

            pairs(pool, halve)

        @block.vector
        def _(dve):
            vec = nc.vector
            chain = Chain(dve, norm_step.sem, norm_step.per)
            carrier = Carrier(dve, dve_waited)

            def norm(i, m, r):
                chain.start(i)
                dve.wait_ge(halved.sem, halved.at(i))
                chain.step(vec.tensor_tensor(rows[:, m, :, 0:D], rows[:, m, :, 0:D], rows[:, m, :, D:2 * D], ALU.add))
                vec.tensor_tensor(res[:, m, :, :], res[:, m, :, :], rows[:, m, :, 0:D], ALU.add).then_inc(summed.sem, 1)
                dve.wait_ge(summed.sem, summed.at(i))
                for t in range(NT):
                    last = vec.bn_stats(st[:, t, :], res[:, m, t, :])
                chain.step(last)
                carrier.take()
                for t in range(NT):
                    last = vec.bn_aggr(mv[:, t, :], st[:, t, :])
                last.then_inc(variance_ready.sem, 1)
                chain.end()
                dve.wait_ge(deviation_ready.sem, deviation_ready.at(i))
                if later(i, 2):
                    dve.wait_ge(stored[m].sem, stored[m].at(r - 1))
                for t in range(NT):
                    last = vec.tensor_scalar(fin[:, m, t, :], res[:, m, t, :], mv[:, t, 0:1], mv[:, t, 1:2],
                                             ALU.subtract, ALU.mult)
                last.then_inc(normed.sem, 1)

            pairs(dve, norm)

        @block.scalar
        def _(act):
            def store(i, m, r):
                act.wait_ge(normed.sem, normed.at(i))
                act.dma_start(out[bass.ds(i * T, T), :].rearrange("(t p) d -> p t d", p=P), fin[:, m, :, :]
                              ).then_inc(stored[m].sem, 16)

            pairs(act, store)
            for m in range(2):
                if nseq > m:
                    act.wait_ge(stored[m].sem, stored[m].at((nseq - 1 - m) // 2))


def host_arrays(i):
    def a(name):
        return np.asarray(i[name])

    x = a("L0_attn_x").reshape(-1, D)
    pad = FJ * P - FH
    s_gu = np.stack([np.pad(a(f"L0_ffn_s_{n}"), (0, pad)).reshape(FJ, P).T for n in ("gate", "up")], 1)
    return {
        "x": x, "xT": x.T,
        "w_in": a("L0_attn_W_in"), "w_out": a("L0_attn_W_out"),
        "a_log": np.broadcast_to(a("L0_attn_A_log"), (P, H)),
        "dt_bias": np.broadcast_to(a("L0_attn_dt_bias"), (P, H)),
        "bc_bias": np.broadcast_to(np.concatenate([a("L0_attn_B_norm_bias"), a("L0_attn_C_norm_bias")], 0), (P, 2, N)),
        "w_gate": a("L0_ffn_wq_gate").T, "w_up": a("L0_ffn_wq_up").T, "w_down": a("L0_ffn_wq_down").T,
        "s_gu": s_gu, "s_down": np.broadcast_to(a("L0_ffn_s_down"), (P, D)),
        "w_qkv": a("L1_attn_w_qkv").T, "w_sw": a("L1_attn_w_swiglu").T, "w_so": a("L1_attn_w_out").T,
        "w_route": a("L1_ffn_gate_inp").T,
        "w_ug": np.concatenate([a("L1_ffn_W_up").transpose(0, 2, 1), a("L1_ffn_W_gate").transpose(0, 2, 1)], 2),
        "w_dn": a("L1_ffn_W_down").transpose(0, 2, 1),
        "matrices": constant_matrices(), "small": small_constants(tile_count(x.shape[0])),
    }


def kernel(**inputs):
    import concourse.bacc as _bacc
    from concourse.bass_utils import run_bass_kernel_spmd as _run

    arrays = {f"in_{n}": np.ascontiguousarray(v) for n, v in host_arrays(inputs).items()}
    nc = _bacc.Bacc("TRN2", target_bir_lowering=False, num_devices=1)
    args = {n[3:]: nc.dram_tensor(n, v.shape, mybir.dt.from_np(v.dtype), kind="ExternalInput").ap()
            for n, v in arrays.items()}
    shape = np.asarray(inputs["L0_attn_x"]).shape
    out = nc.dram_tensor("out", [shape[0] * shape[1], D], F32, kind="ExternalOutput").ap()
    build(nc, args, out)
    r = _run(nc, [arrays], core_ids=[0])
    return r.results[0]["out"].reshape(shape)
```

```python
from contextlib import ExitStack

import numpy as np

import concourse.bass as bass
from concourse import mybir

F32 = mybir.dt.float32
BF16 = mybir.dt.bfloat16
I32 = mybir.dt.int32
U32 = mybir.dt.uint32
ALU = mybir.AluOpType
ACT = mybir.ActivationFunctionType
AX_X = mybir.AxisListType.X

P = 128
T = 256
NT = T // P
D = 256
DC = D // P
DI = 512
H = 64
HD = DI // H
N = 64
REST = 2 * N + 2 * H + N // 2
LV = 7
FH = 704
FJ = (FH + P - 1) // P
SH = 1024
SJ = SH // P
NE = 16
TOPK = 4
EH = 448
EC = 112
EJ = EH // EC
UN = 8
US = 4
MAGIC = 1.5 * 2.0 ** 23
LN_EPS = 1e-5
RMS_EPS = 1.1920929e-07
TWO_PI_HI = 6.28125
TWO_PI_LO = 2.0 * np.pi - 6.28125
DT_MIN, DT_MAX = 0.0001, 0.5
DVE_A, DVE_B = 20, 16

SUFFIX, PREFIX, STRICT, ONES, SHIFT, EDGE, IDENT = range(LV, LV + 7)
MASK0 = LV + 7


def constant_matrices():
    r, c = np.arange(P)[:, None], np.arange(P)[None, :]
    m = np.zeros((P, MASK0 + LV, P), np.float32)
    for k in range(LV):
        half = 2 ** k
        same = r // (2 * half) == c // (2 * half)
        right_r, right_c = r // half % 2 == 1, c // half % 2 == 1
        m[:, k] = same & np.where(right_c, right_r & (r <= c), ~right_r & (r > c))
        m[:, MASK0 + k] = same & ~right_r & right_c
    m[:, SUFFIX] = r > c
    m[:, PREFIX] = r <= c
    m[:, STRICT] = r < c
    m[:, ONES] = 1
    m[:, SHIFT] = r == c + 1
    m[:, EDGE] = (r == 0) & (c == P - 1)
    m[:, IDENT] = r == c
    return m


def tile_count(tokens):
    most = (tokens * TOPK + NE * (P - 1) + NE - 1) // P
    return -(-most // UN) * UN


class Signal:

    def __init__(self, sem, per):
        self.sem, self.per = sem, per

    def at(self, s, k=None):
        return s * self.per + (self.per if k is None else k)

    def before(self, s):
        return s * self.per


def later(s, n=1):
    return not isinstance(s, int) or s >= n


class Carrier:

    def __init__(self, eng, sem):
        self.eng, self.sem = eng, sem

    def take(self):
        self.eng.sem_inc(self.sem, 1)


class Chain:

    def __init__(self, eng, sem, per):
        self.eng, self.sem, self.per, self.k, self.s = eng, sem, per, 0, 0

    def start(self, s):
        self.s, self.k = s, 0

    def go_on(self, s):
        self.s = s

    def step(self, ins):
        self.k += 1
        ins.then_inc(self.sem, 1)
        self.eng.wait_ge(self.sem, self.s * self.per + self.k)

    def end(self):
        assert self.k == self.per, (self.k, self.per)


def spread(ap, axis, n):
    a = ap.unsqueeze(axis)
    shape = list(a.shape)
    shape[axis] = n
    return a.broadcast_to(shape)


ORDER = (["F1", "D8", "F2", "B1T", "F4.0", "C7", "B1.0", "C7L", "B1.1", "F4.1", "B1.2", "F4.2", "B1.3", "B1.4"]
         + ["C8", "B1.5", "A2", "B2", "F3", "N0", "A3", "B2L", "B3T", "A2L", "AU.0", "AU.1", "AU.2", "AU.3", "A3L", "B3"]
         + ["A4.0", "A4.1", "B4", "A4.2", "AU.4", "A4.3", "AU.5", "B5T", "B5.0", "B5.1", "A4.4", "AU.6"]
         + ["B5.2", "A4.5", "AU.7", "B5.3", "A4.6", "B5.4", "A4.7", "B5.5", "B5.6", "B5.7", "B6.0", "A5", "B6.1", "A6"])
SHIFT_OF = {"N": 1, "F": 0, "A": 0, "B": -1, "C": -2, "D": -3}


def run_skewed(eng, nseq, pieces):

    def one_round(i):
        for name in ORDER:
            s = i + SHIFT_OF[name[0]]
            whole, _, k = name.partition(".")
            if whole in pieces and (not isinstance(i, int) or 0 <= s < nseq):
                pieces[whole](s, *([int(k)] if k else []))

    first, end = 3, max(3, nseq - 1)
    for i in range(-1, first):
        one_round(i)
    if end > first:
        with eng.Fori(first, end) as i:
            one_round(i)
    for i in range(end, nseq + 3):
        one_round(i)


def build(nc, ins, out):
    nseq = ins["x"].shape[0] // T
    ntok = nseq * T
    cap = ntok + P
    ntile = tile_count(ntok)
    nslot = (NE + 1) * cap

    meta_dram = nc.dram_tensor("meta_dram", [nslot, 4], U32).ap()
    x3_dram = nc.dram_tensor("x3_dram", [ntok, D], F32).ap()
    yk_dram = nc.dram_tensor("yk_dram", [ntok * TOPK, D], F32).ap()

    with ExitStack() as whole:
        ident = whole.enter_context(nc.sbuf_tensor("ident", [P, P], F32))
        small = whole.enter_context(nc.sbuf_tensor("small", [P, ins["small"].shape[1]], F32))
        base = whole.enter_context(nc.sbuf_tensor("base", [P, NE], F32))
        layers_block(nc, ins, nseq, cap, ident, small, base, meta_dram, x3_dram)
        experts_block(nc, ins, ntok, cap, ntile, ident, small, base, meta_dram, x3_dram, yk_dram)
        combine_block(nc, nseq, x3_dram, yk_dram, out)


SM_P, SM_E, SM_DST, SM_TRI, SM_I = 0, 1, 1 + NE, 1 + NE + NT * TOPK, 1 + NE + NT * TOPK + NE * NE


def small_constants(ntile):
    s = np.zeros((P, SM_I + ntile), np.float32)
    p = np.arange(P)
    s[:, SM_P] = p
    s[:, SM_E:SM_DST] = np.arange(NE)
    dst = (np.arange(NT)[None, :, None] * P + p[:, None, None]) * TOPK + np.arange(TOPK)[None, None, :]
    s[:, SM_DST:SM_TRI] = dst.reshape(P, -1)
    s[:, SM_TRI:SM_I] = np.tril(np.ones((NE, NE))).reshape(1, -1)
    s[:, SM_I:] = np.arange(ntile)
    return s


def layers_block(nc, ins, nseq, cap, ident, small, base, meta_dram, x3_dram):
    with ExitStack() as ctx:
        def sb(name, shape, dt=F32):
            return ctx.enter_context(nc.sbuf_tensor(name, shape, dt))

        def sig(name, per):
            return Signal(ctx.enter_context(nc.semaphore(name)), per)

        const = sb("const", [P, MASK0 + LV, P])
        w_in = sb("w_in", [P, DC, 2 * DI + REST])
        w_out = sb("w_out", [P, DI // P, D])
        w_gate = sb("w_gate", [P, DC, FH])
        w_up = sb("w_up", [P, DC, FH])
        w_down = sb("w_down", [P, FJ, D])
        s_gu = sb("s_gu", [P, 2, FJ])
        s_down = sb("s_down", [P, D])
        w_qkv = sb("w_qkv", [P, DC, 3 * D])
        w_sw = sb("w_sw", [P, DC, 2 * SH])
        w_so = sb("w_so", [P, SJ, D])
        w_route = sb("w_route", [P, DC, NE])
        dt_bias = sb("dt_bias", [P, H])
        neg_a = sb("neg_a", [P, H])
        bc_bias = sb("bc_bias", [P, 2, N])

        xT = sb("xT", [P, DC, T])
        x_row = sb("x_row", [P, NT, D])
        rest = sb("rest", [P, NT, REST])
        xs = sb("xs", [P, NT, DI])
        zs = sb("zs", [P, NT, DI])
        vl = sb("vl", [P, NT, 2 * H])
        eu = sb("eu", [P, NT, 2 * H])
        rec = sb("rec", [P, NT, 2 * H])
        lnw = sb("lnw", [P, NT, H])
        dt = sb("dt", [P, NT, H])
        d_a = sb("d_a", [P, NT, H])
        ld = sb("ld", [P, NT, H])
        q = sb("q", [P, NT, H])
        g = sb("g", [P, NT, H])
        coef = sb("coef", [P, NT, H])
        dtm = sb("dtm", [P, NT])
        power = sb("power", [P, 4])
        dth = sb("dth", [P, NT, N // 2])
        bcn = sb("bcn", [P, NT, 2, N])
        bct = sb("bct", [P, NT, 2, N])
        bcu = sb("bcu", [P, NT, 2, N])
        bcr = sb("bcr", [P, NT, 2, N])
        ssq = sb("ssq", [P, NT, 2])
        ang = sb("ang", [P, NT, 2, N // 2])
        turns = sb("turns", [P, NT, 2, N // 2])
        cs = sb("cs", [P, NT, 2, N // 2])
        cb = sb("cb", [P, NT])
        bcT = sb("bcT", [N, NT, 2, P])
        decay = sb("decay", [P, LV + 1, NT, H])
        masked = sb("masked", [P, NT, LV, P])
        cb_all = sb("cb_all", [P, NT + 1, P])
        xg = sb("xg", [P, NT, DI])
        u = sb("u", [P, US, NT, DI])
        v = sb("v", [P, 2, NT, DI])
        y = sb("y", [P, NT, DI])
        ynT = sb("ynT", [P, NT, DI // P, P])
        sq_a = sb("sq_a", [P, DI])
        yss = sb("yss", [P, NT])
        r1 = sb("r1", [P, NT, D])
        st1 = sb("st1", [P, NT, 6])
        mv1 = sb("mv1", [P, NT, 2])

        x1 = sb("x1", [P, NT, D])
        x1T = sb("x1T", [P, DC, T])
        sg = sb("sg", [P, 2, T])
        hT = sb("hT", [P, SJ, T])
        x2 = sb("x2", [P, NT, D])
        r2 = sb("r2", [P, NT, D])
        st2 = sb("st2", [P, NT, 6])
        mv2 = sb("mv2", [P, NT, 2])
        x2n = sb("x2n", [P, NT, D])
        sq_b = sb("sq_b", [P, D])
        scales = sb("scales", [P, 2 * NT])
        qk_ss = sb("qk_ss", [P, NT, 2])
        eq = sb("eq", [P, NT, D])
        wv = sb("wv", [P, NT, 2, D])
        den = sb("den", [P, NT, D])
        yc = sb("yc", [P, NT, D])
        x3 = sb("x3", [P, NT, D])
        x3T = sb("x3T", [P, DC, T])
        logits = sb("logits", [P, NT, NE])
        top = sb("top", [P, NT, 8])
        topi = sb("topi", [P, NT, 8], U32)
        topf = sb("topf", [P, NT, TOPK])
        ez = sb("ez", [P, NT, TOPK])
        esum = sb("esum", [P, NT])
        hot = sb("hot", [P, NT, TOPK, NE])
        hot_pos = sb("hot_pos", [P, NT, TOPK, NE])
        chosen = sb("chosen", [P, NT, NE])
        pos = sb("pos", [P, NT, NE])
        slot_f = sb("slot_f", [P, NT, TOPK])
        slot = sb("slot", [P, NT, TOPK], U32)
        dst = sb("dst", [P, NT, TOPK])
        tok = sb("tok", [P, NT])
        meta = sb("meta", [P, NT, TOPK, 4], U32)
        padding = sb("padding", [P, cap // P, 4], U32)

        pa = ctx.enter_context(nc.psum_tensor("pa", [P, 4, 512], F32))
        pb = ctx.enter_context(nc.psum_tensor("pb", [P, 4, 512], F32))
        ident = ident[:, :]

        def mat(k):
            return const[:, k, :]

        loads = [(const[:, :, :], ins["matrices"]), (ident, ins["matrices"][:, IDENT, :]), (small[:, :], ins["small"]),
                 (w_in[:, :, :], ins["w_in"].rearrange("(c p) n -> p c n", p=P)),
                 (dt_bias[:, :], ins["dt_bias"]), (neg_a[:, :], ins["a_log"]),
                 (bc_bias[:, :, :], ins["bc_bias"]),
                 (w_out[:, :, :], ins["w_out"].rearrange("(c p) n -> p c n", p=P))]
        loads_b = [(w_gate[:, :, :].bitcast(I32), ins["w_gate"].rearrange("(c p) n -> p c n", p=P)),
                   (w_up[:, :, :].bitcast(I32), ins["w_up"].rearrange("(c p) n -> p c n", p=P)),
                   (w_down[:, 0:FJ - 1, :].bitcast(I32),
                    ins["w_down"][0:(FJ - 1) * P, :].rearrange("(c p) n -> p c n", p=P)),
                   (w_down[0:FH - (FJ - 1) * P, FJ - 1, :].bitcast(I32), ins["w_down"][(FJ - 1) * P:FH, :]),
                   (s_gu[:, :, :], ins["s_gu"]), (s_down[:, :], ins["s_down"]),
                   (w_qkv[:, :, :], ins["w_qkv"].rearrange("(c p) n -> p c n", p=P)),
                   (w_sw[:, :, :], ins["w_sw"].rearrange("(c p) n -> p c n", p=P)),
                   (w_so[:, :, :], ins["w_so"].rearrange("(c p) n -> p c n", p=P)),
                   (w_route[:, :, :], ins["w_route"].rearrange("(c p) n -> p c n", p=P))]
        setup_loaded = sig("setup_loaded", 16 * len(loads))
        weights_loaded = sig("weights_loaded", 16 * len(loads_b))
        dequantised = sig("dequantised", 6)
        setup_done = sig("setup_done", 1)
        padding_set = sig("padding_set", 1)
        padding_stored = sig("padding_stored", 16 * (NE + 1))
        a_exp = sig("a_exp", 1)

        xT_in = sig("xT_in", 16)
        x_row_in = sig("x_row_in", 16)
        rest_projected = sig("rest_projected", NT)
        x_projected = sig("x_projected", NT)
        z_projected = sig("z_projected", NT)
        rest_copied = sig("rest_copied", NT)
        xs_ready = sig("xs_ready", NT)
        zs_ready = sig("zs_ready", NT)
        v_ready = sig("v_ready", 1)
        eu_ready = sig("eu_ready", 1)
        w_ready = sig("w_ready", 1)
        ln_ready = sig("ln_ready", 1)
        steps_ready = sig("steps_ready", 1)
        shifted = sig("shifted", 1)
        decay_sums = sig("decay_sums", 1)
        decay_ready = sig("decay_ready", 1)
        ang_ready = sig("ang_ready", 1)
        sin_ready = sig("sin_ready", 1)
        g_ready = sig("g_ready", 1)
        roped = sig("roped", 1)
        coef_ready = sig("coef_ready", 1)
        bc_transposed = sig("bc_transposed", 1)
        bcT_ready = sig("bcT_ready", 1)
        cb_ready = sig("cb_ready", 1)
        masked_ready = sig("masked_ready", 2 * NT)
        cb_copied = sig("cb_copied", 1)
        xg_ready = sig("xg_ready", 1)
        u_ready = sig("u_ready", LV + 1)
        level_done = sig("level_done", LV + 1)
        v_scaled = sig("v_scaled", LV + 1)
        y_added = sig("y_added", LV + 2)
        yss_ready = sig("yss_ready", NT)
        yn_ready = sig("yn_ready", NT)
        yn_transposed = sig("yn_transposed", NT)
        ynT_ready = sig("ynT_ready", NT)
        out_projected = sig("out_projected", 1)
        x1_ready = sig("x1_ready", NT)
        bc_squares, bc_rms, y_rms = (sig(n, 1) for n in ("bc_squares", "bc_rms", "y_rms"))
        norm1, norm2, norm3 = ((sig(f"variance{n}", 1), sig(f"deviation{n}", 1)) for n in (1, 2, 3))
        power_set = sig("power_set", 1)
        pool_waited, dve_waited, pe_waited = (ctx.enter_context(nc.semaphore(f"{n}_waited")) for n in ("pool", "dve", "pe"))
        pool_a = sig("pool_a", 3)
        pool_b = sig("pool_b", 4)
        dve_a = sig("dve_a", DVE_A)

        x1_transposed = sig("x1_transposed", 1)
        x1T_ready = sig("x1T_ready", 1)
        ffn_projected = sig("ffn_projected", FJ)
        ffn_silu = sig("ffn_silu", FJ)
        ffn_h = sig("ffn_h", FJ)
        ffn_out = sig("ffn_out", 1)
        x2_ready = sig("x2_ready", NT)
        x2n_ready = sig("x2n_ready", NT)
        x2_transposed = sig("x2_transposed", 1)
        x2T_ready = sig("x2T_ready", 1)
        qk_projected = sig("qk_projected", NT)
        v_projected = sig("v_projected", 1)
        qk_ss_ready = sig("qk_ss_ready", NT * 2)
        qk_rms_ready = sig("qk_rms_ready", 1)
        k_exp = sig("k_exp", NT)
        q_exp = sig("q_exp", NT)
        wv_ready = sig("wv_ready", NT)
        cumulated = sig("cumulated", NT)
        yc_ready = sig("yc_ready", 1)
        yc_transposed = sig("yc_transposed", 1)
        ycT_ready = sig("ycT_ready", 1)
        sw_projected = sig("sw_projected", SJ)
        sw_silu = sig("sw_silu", SJ)
        sw_h = sig("sw_h", SJ)
        sw_out = sig("sw_out", NT)
        x3_ready = sig("x3_ready", NT)
        x3_transposed = sig("x3_transposed", 1)
        x3T_ready = sig("x3T_ready", 1)
        logits_done = sig("logits_done", 1)
        logits_copied = sig("logits_copied", 1)
        gap_ready = sig("gap_ready", 1)
        top_exp = sig("top_exp", 1)
        chosen_ready = sig("chosen_ready", 1)
        counted = sig("counted", 1)
        meta_ready = sig("meta_ready", 1)
        x3_stored = sig("x3_stored", 16)
        meta_stored = sig("meta_stored", 16 * NT * TOPK)
        dve_b = sig("dve_b", DVE_B)

        block = ctx.enter_context(nc.Block())

        @block.sync
        def _(sp):
            for to, src in loads:
                sp.dma_start(to, src).then_inc(setup_loaded.sem, 16)

            def load_x(s):
                if later(s):
                    sp.wait_ge(z_projected.sem, z_projected.before(s))
                sp.dma_start(xT[:, :, :], ins["xT"].rearrange("(c p) t -> p c t", p=P)[:, :, bass.ds(s * T, T)]
                             ).then_inc(xT_in.sem, 16)

            def load_rows(s):
                if later(s):
                    sp.wait_ge(x1_ready.sem, x1_ready.before(s))
                sp.dma_start(x_row[:, :, :], ins["x"][bass.ds(s * T, T), :].rearrange("(t p) d -> p t d", p=P)
                             ).then_inc(x_row_in.sem, 16)
                if isinstance(s, int) and s == 0:
                    for to, src in loads_b:
                        sp.dma_start(to, src).then_inc(weights_loaded.sem, 16)
                    sp.wait_ge(padding_set.sem, padding_set.at(0))
                    for e in range(NE + 1):
                        sp.dma_start(meta_dram[e * cap:(e + 1) * cap, :].rearrange("(p i) w -> p i w", p=P),
                                     padding[:, :, :]).then_inc(padding_stored.sem, 16)

            def store_x3(s):
                sp.wait_ge(x3_ready.sem, x3_ready.at(s))
                sp.dma_start(x3_dram[bass.ds(s * T, T), :].rearrange("(t p) d -> p t d", p=P), x3[:, :, :]
                             ).then_inc(x3_stored.sem, 16)

            run_skewed(sp, nseq, {"N0": load_x, "F1": load_rows, "C7": store_x3})
            sp.wait_ge(x3_stored.sem, x3_stored.at(nseq - 1))

        @block.tensor
        def _(pe):
            mm = nc.tensor.matmul
            pe_carrier = Carrier(pe, pe_waited)

            def project(s, first, width, bank, done):
                for t in range(NT):
                    for c in range(DC):
                        last = mm(pa[:, bank + t, 0:width], xT[:, c, t * P:(t + 1) * P],
                                  w_in[:, c, first:first + width], start=c == 0, stop=c == DC - 1)
                    last.then_inc(done.sem, 1)

            def f1(s):
                if isinstance(s, int) and s == 0:
                    pe.wait_ge(setup_loaded.sem, setup_loaded.at(0))
                pe.wait_ge(xT_in.sem, xT_in.at(s))
                if later(s):
                    pe.wait_ge(ynT_ready.sem, ynT_ready.before(s))
                project(s, 2 * DI, REST, 0, rest_projected)

            def f2(s):
                if later(s):
                    pe.wait_ge(norm1[0].sem, norm1[0].before(s))
                project(s, DI, DI, 2, x_projected)

            def f3(s):
                pe.wait_ge(rest_copied.sem, rest_copied.at(s))
                project(s, 0, DI, 0, z_projected)

            def a2(s):
                pe.wait_ge(steps_ready.sem, steps_ready.at(s))
                pe.wait_ge(xs_ready.sem, xs_ready.at(s, 1))
                mm(pa[:, 2, 0:H], mat(SHIFT), q[:, 0, :], start=True, stop=False)
                mm(pa[:, 2, 0:H], mat(EDGE), q[:, 1, :], start=False, stop=True)
                mm(pa[:, 2, H:2 * H], mat(SHIFT), q[:, 1, :], start=True, stop=True)
                o = 2 * H
                mm(pa[:, 2, o:o + N // 2], mat(PREFIX), dth[:, 0, :], start=True, stop=True)
                o += N // 2
                mm(pa[:, 2, o:o + N // 2], mat(PREFIX), dth[:, 1, :], start=True, stop=False)
                mm(pa[:, 2, o:o + N // 2], mat(ONES), dth[:, 0, :], start=False, stop=True).then_inc(shifted.sem, 1)

            def a2_late(s):
                pe.wait_ge(zs_ready.sem, zs_ready.at(s))
                for k in range(LV):
                    mm(pa[:, k // 4, k % 4 * P:(k % 4 + 1) * P], mat(k), d_a[:, :, :].rearrange("p t h -> p (t h)"),
                       start=True, stop=True)
                mm(pa[:, 1, 3 * P:3 * P + H], mat(SUFFIX), d_a[:, 0, :], start=True, stop=True)
                mm(pa[:, 1, 3 * P + H:4 * P], mat(PREFIX), d_a[:, 1, :], start=True, stop=True
                   ).then_inc(decay_sums.sem, 1)

            def a3(s):
                pe.wait_ge(roped.sem, roped.at(s))
                pe.wait_ge(xs_ready.sem, xs_ready.at(s))
                pe_carrier.take()
                for t in range(NT):
                    for m in range(2):
                        last = nc.tensor.transpose(pa[0:N, 3, (2 * t + m) * P:(2 * t + m + 1) * P],
                                                   bcr[:, t, m, :], ident)
                last.then_inc(bc_transposed.sem, 1)

            def a3_late(s):
                pe.wait_ge(bcT_ready.sem, bcT_ready.at(s))
                pe.wait_ge(g_ready.sem, g_ready.at(s))
                for n, (tb, tc) in enumerate(((0, 0), (1, 1), (0, 1))):
                    last = mm(pa[:, 2, n * P:(n + 1) * P], bcT[:, tb, 0, :], bcT[:, tc, 1, :], start=True, stop=True)
                last.then_inc(cb_ready.sem, 1)

            def a4(s, k):
                if k == 0:
                    pe.wait_ge(decay_ready.sem, decay_ready.at(s))
                    pe.wait_ge(masked_ready.sem, masked_ready.at(s, NT))
                    pe.wait_ge(cb_copied.sem, cb_copied.at(s))
                elif k == 2:
                    pe.wait_ge(masked_ready.sem, masked_ready.at(s))
                pe.wait_ge(u_ready.sem, u_ready.at(s, k + 1))
                if k >= 2:
                    pe.wait_ge(v_scaled.sem, v_scaled.at(s, k - 1))
                if k < LV:
                    for t in range(NT):
                        last = mm(pa[:, 2 * (k % 2) + t, :], masked[:, t, k, :], u[:, k % US, t, :],
                                  start=True, stop=True)
                else:
                    last = mm(pa[:, 2 * (k % 2) + 1, :], cb_all[:, 2, :], u[:, k % US, 0, :], start=True, stop=True)
                last.then_inc(level_done.sem, 1)

            def a5(s):
                for t in range(NT):
                    pe.wait_ge(yn_ready.sem, yn_ready.at(s, t + 1))
                    for c in range(DI // P):
                        last = nc.tensor.transpose(pa[:, t, c * P:(c + 1) * P], y[:, t, c * P:(c + 1) * P], ident)
                    last.then_inc(yn_transposed.sem, 1)

            def a6(s):
                for t in range(NT):
                    pe.wait_ge(ynT_ready.sem, ynT_ready.at(s, t + 1))
                    for c in range(DI // P):
                        last = mm(pa[:, 2, t * D:(t + 1) * D], ynT[:, t, c, :], w_out[:, c, :],
                                  start=c == 0, stop=c == DI // P - 1)
                last.then_inc(out_projected.sem, 1)
                if isinstance(s, int) and s == 0:
                    pe.wait_ge(dequantised.sem, dequantised.at(0))
                    pe.wait_ge(weights_loaded.sem, weights_loaded.at(0))

            def transposes(rows, ready, done, s, bank=0):
                pe.wait_ge(ready.sem, ready.at(s))
                for c in range(DC):
                    for t in range(NT):
                        last = nc.tensor.transpose(pb[:, bank, c * T + t * P:c * T + (t + 1) * P],
                                                   rows[:, t, c * P:(c + 1) * P], ident)
                last.then_inc(done.sem, 1)

            def b1_first(s):
                transposes(x1, x1_ready, x1_transposed, s)

            def b1(s, j):
                if j == 0:
                    pe.wait_ge(x1T_ready.sem, x1T_ready.at(s))
                rows = min(P, FH - j * P)
                if j >= 2:
                    pe.wait_ge(ffn_h.sem, ffn_h.at(s, j - 1))
                for w, weight in enumerate((w_gate, w_up)):
                    for c in range(DC):
                        last = mm(pb[0:rows, 1 + j % 2, w * T:(w + 1) * T], weight[:, c, j * P:j * P + rows],
                                  x1T[:, c, :], start=c == 0, stop=c == DC - 1)
                last.then_inc(ffn_projected.sem, 1)

            def b2(s):
                if later(s):
                    pe.wait_ge(meta_ready.sem, meta_ready.before(s))
                pe.wait_ge(ffn_h.sem, ffn_h.at(s, FJ - 1))
                for t in range(NT):
                    for j in range(FJ):
                        if t == 0 and j == FJ - 1:
                            pe.wait_ge(ffn_h.sem, ffn_h.at(s))
                        rows = min(P, FH - j * P)
                        last = mm(pb[:, 3, t * D:(t + 1) * D], hT[0:rows, j, t * P:(t + 1) * P], w_down[0:rows, j, :],
                                  start=j == 0, stop=j == FJ - 1)
                last.then_inc(ffn_out.sem, 1)

            def b3_first(s):
                transposes(x2n, x2n_ready, x2_transposed, s)

            def b3(s):
                pe.wait_ge(x2T_ready.sem, x2T_ready.at(s))
                for t in range(NT):
                    for c in range(DC):
                        last = mm(pb[:, 1 + t, :], x1T[:, c, t * P:(t + 1) * P], w_qkv[:, c, 0:2 * D],
                                  start=c == 0, stop=c == DC - 1)
                    last.then_inc(qk_projected.sem, 1)
                for t in range(NT):
                    for c in range(DC):
                        last = mm(pb[:, 3, t * D:(t + 1) * D], x1T[:, c, t * P:(t + 1) * P], w_qkv[:, c, 2 * D:3 * D],
                                  start=c == 0, stop=c == DC - 1)
                last.then_inc(v_projected.sem, 1)

            def b4(s):
                pe.wait_ge(q_exp.sem, q_exp.at(s))
                for t in range(NT):
                    pe.wait_ge(wv_ready.sem, wv_ready.at(s, t + 1))
                    rhs = wv[:, t, :, :].rearrange("p a d -> p (a d)")
                    last = mm(pb[:, 1 + t, :], mat(PREFIX), rhs, start=True, stop=t == 0)
                    if t == 1:
                        last = mm(pb[:, 1 + t, :], mat(ONES), wv[:, 0, :, :].rearrange("p a d -> p (a d)"),
                                  start=False, stop=True)
                    last.then_inc(cumulated.sem, 1)

            def b5_first(s):
                transposes(yc, yc_ready, yc_transposed, s)

            def b5(s, j):
                if j == 0:
                    pe.wait_ge(ycT_ready.sem, ycT_ready.at(s))
                if j >= 2:
                    pe.wait_ge(sw_h.sem, sw_h.at(s, j - 1))
                for w in range(2):
                    for c in range(DC):
                        o = (1 - w) * SH + j * P
                        last = mm(pb[:, 1 + j % 2, w * T:(w + 1) * T], w_sw[:, c, o:o + P], x1T[:, c, :],
                                  start=c == 0, stop=c == DC - 1)
                last.then_inc(sw_projected.sem, 1)

            def b6(s, t):
                for j in range(SJ):
                    if t == 0 and j in (0, SJ - 1):
                        pe.wait_ge(sw_h.sem, sw_h.at(s, SJ if j else SJ - 1))
                    last = mm(pb[:, 3, t * D:(t + 1) * D], hT[:, j, t * P:(t + 1) * P], w_so[:, j, :],
                              start=j == 0, stop=j == SJ - 1)
                last.then_inc(sw_out.sem, 1)

            def c7(s):
                transposes(x3, x3_ready, x3_transposed, s, 3)

            def c7_late(s):
                pe.wait_ge(x3T_ready.sem, x3T_ready.at(s))
                for t in range(NT):
                    for c in range(DC):
                        last = mm(pb[:, 3, t * NE:(t + 1) * NE], x3T[:, c, t * P:(t + 1) * P], w_route[:, c, :],
                                  start=c == 0, stop=c == DC - 1)
                last.then_inc(logits_done.sem, 1)

            def c8(s):
                pe.wait_ge(chosen_ready.sem, chosen_ready.at(s))
                mm(pb[:, 3, 0:NE], mat(STRICT), chosen[:, 0, :], start=True, stop=True)
                mm(pb[:, 3, NE:2 * NE], mat(STRICT), chosen[:, 1, :], start=True, stop=False)
                mm(pb[:, 3, NE:2 * NE], mat(ONES), chosen[:, 0, :], start=False, stop=True)
                mm(pb[:, 3, 2 * NE:3 * NE], mat(ONES), chosen[:, 0, :], start=True, stop=False)
                mm(pb[:, 3, 2 * NE:3 * NE], mat(ONES), chosen[:, 1, :], start=False, stop=True
                   ).then_inc(counted.sem, 1)

            run_skewed(pe, nseq, {"F1": f1, "F2": f2, "F3": f3, "A2": a2, "A2L": a2_late, "A3": a3, "A3L": a3_late,
                                  "A4": a4, "A5": a5, "A6": a6, "B1T": b1_first, "B1": b1, "B2": b2, "B3T": b3_first,
                                  "B3": b3, "B4": b4, "B5T": b5_first, "B5": b5, "B6": b6, "C7": c7, "C7L": c7_late, "C8": c8})

        @block.scalar
        def _(act):
            act_f = nc.scalar.activation
            act.wait_ge(setup_loaded.sem, setup_loaded.at(0))
            act_f(neg_a[:, :], neg_a[:, :], ACT.Exp).then_inc(a_exp.sem, 1)

            def f1(s):
                for t in range(NT):
                    act.wait_ge(rest_projected.sem, rest_projected.at(s, t + 1))
                    act_f(rest[:, t, :], pa[:, t, 0:REST], ACT.Copy).then_inc(rest_copied.sem, 1)

            def f2(s):
                act.wait_ge(v_ready.sem, v_ready.at(s))
                act_f(eu[:, :, :], vl[:, :, :], ACT.Exp).then_inc(eu_ready.sem, 1)

            def f4(s, k):
                if k == 0:
                    act.wait_ge(w_ready.sem, w_ready.at(s))
                    act_f(lnw[:, :, :], vl[:, :, 0:H], ACT.Ln).then_inc(ln_ready.sem, 1)
                if k != 1:
                    return
                for t in range(NT):
                    act.wait_ge(x_projected.sem, x_projected.at(s, t + 1))
                    act_f(xs[:, t, :], pa[:, 2 + t, :], ACT.Silu).then_inc(xs_ready.sem, 1)

            def f3(s):
                for t in range(NT):
                    act.wait_ge(z_projected.sem, z_projected.at(s, t + 1))
                    act_f(zs[:, t, :], pa[:, t, :], ACT.Silu).then_inc(zs_ready.sem, 1)

            def a2(s):
                act.wait_ge(ang_ready.sem, ang_ready.at(s))
                act_f(cs[:, :, :, :], ang[:, :, :, :], ACT.Sin).then_inc(sin_ready.sem, 1)

            def a2_late(s):
                act.wait_ge(decay_sums.sem, decay_sums.at(s))
                act_f(decay[:, :, :, :].rearrange("p k t h -> p (k t h)"),
                      pa[:, 0:2, :].rearrange("p b n -> p (b n)"), ACT.Exp).then_inc(decay_ready.sem, 1)

            def a3(s):
                act.wait_ge(bc_transposed.sem, bc_transposed.at(s))
                act_f(bcT[:, :, :, :].rearrange("n t m l -> n (t m l)"), pa[0:N, 3, :], ACT.Copy
                      ).then_inc(bcT_ready.sem, 1)

            def a3_late(s):
                act.wait_ge(cb_ready.sem, cb_ready.at(s))
                act_f(cb_all[:, :, :].rearrange("p a b -> p (a b)"), pa[:, 2, 0:3 * P], ACT.Copy
                      ).then_inc(cb_copied.sem, 1)

            def a5(s):
                act.wait_ge(y_added.sem, y_added.at(s))
                for t in range(NT):
                    act_f(sq_a[:, :], y[:, t, :], ACT.Square, accum_out=yss[:, t:t + 1]).then_inc(yss_ready.sem, 1)
                    act.wait_ge(yss_ready.sem, yss_ready.at(s, t + 1))
                for t in range(NT):
                    act.wait_ge(yn_transposed.sem, yn_transposed.at(s, t + 1))
                    act_f(ynT[:, t, :, :].rearrange("p c l -> p (c l)"), pa[:, t, :], ACT.Copy
                          ).then_inc(ynT_ready.sem, 1)
                if isinstance(s, int) and s == 0:
                    act.wait_ge(weights_loaded.sem, weights_loaded.at(0))

            def transposed(done, ready, s, to=x1T, bank=0):
                act.wait_ge(done.sem, done.at(s))
                act_f(to[:, :, :].rearrange("p c t -> p (c t)"), pb[:, bank, :], ACT.Copy).then_inc(ready.sem, 1)

            def b1_first(s):
                transposed(x1_transposed, x1T_ready, s)

            def b1(s, j):
                rows = min(P, FH - j * P)
                act.wait_ge(ffn_projected.sem, ffn_projected.at(s, j + 1))
                if j >= 2:
                    act.wait_ge(ffn_h.sem, ffn_h.at(s, j - 1))
                act_f(sg[0:rows, j % 2, :], pb[0:rows, 1 + j % 2, 0:T], ACT.Silu,
                      scale=s_gu[0:rows, 0, j:j + 1]).then_inc(ffn_silu.sem, 1)

            def b3_first(s):
                transposed(x2_transposed, x2T_ready, s)

            def b3(s):
                for t in range(NT):
                    act.wait_ge(qk_projected.sem, qk_projected.at(s, t + 1))
                    for m in range(2):
                        act_f(sq_b[:, :], pb[:, 1 + t, m * D:(m + 1) * D], ACT.Square,
                              accum_out=qk_ss[:, t, m:m + 1]).then_inc(qk_ss_ready.sem, 1)
                        act.wait_ge(qk_ss_ready.sem, qk_ss_ready.at(s, 2 * t + m + 1))
                act.wait_ge(qk_rms_ready.sem, qk_rms_ready.at(s))
                for t in range(NT):
                    act_f(wv[:, t, 0, :], pb[:, 1 + t, D:2 * D], ACT.Exp, scale=qk_ss[:, t, 1:2]
                          ).then_inc(k_exp.sem, 1)
                for t in range(NT):
                    act_f(eq[:, t, :], pb[:, 1 + t, 0:D], ACT.Exp, scale=qk_ss[:, t, 0:1]).then_inc(q_exp.sem, 1)

            def b5_first(s):
                transposed(yc_transposed, ycT_ready, s)

            def b5(s, j):
                act.wait_ge(sw_projected.sem, sw_projected.at(s, j + 1))
                if j >= 2:
                    act.wait_ge(sw_h.sem, sw_h.at(s, j - 1))
                act_f(sg[:, j % 2, :], pb[:, 1 + j % 2, 0:T], ACT.Silu).then_inc(sw_silu.sem, 1)

            def c7(s):
                transposed(x3_transposed, x3T_ready, s, x3T, 3)

            def c7_late(s):
                act.wait_ge(logits_done.sem, logits_done.at(s))
                act_f(logits[:, :, :].rearrange("p t e -> p (t e)"), pb[:, 3, 0:NT * NE], ACT.Copy
                      ).then_inc(logits_copied.sem, 1)

            def c8(s):
                act.wait_ge(gap_ready.sem, gap_ready.at(s))
                act_f(ez[:, :, :], ez[:, :, :], ACT.Exp).then_inc(top_exp.sem, 1)

            run_skewed(act, nseq, {"F1": f1, "F2": f2, "F3": f3, "F4": f4, "A2": a2, "A2L": a2_late, "A3": a3,
                                   "A3L": a3_late, "A5": a5, "B1T": b1_first, "B1": b1, "B3T": b3_first, "B3": b3, "B5T": b5_first,
                                   "B5": b5, "C7": c7, "C7L": c7_late, "C8": c8})

        @block.gpsimd
        def _(pool):
            carrier = Carrier(pool, pool_waited)
            pa_ = Chain(pool, pool_a.sem, pool_a.per)
            pb_ = Chain(pool, pool_b.sem, pool_b.per)

            nc.gpsimd.memset(padding[:, :, 1:4], 0)
            nc.gpsimd.memset(padding[:, :, 0:1], 2 ** 30).then_inc(padding_set.sem, 1)
            nc.gpsimd.memset(power[:, :], -0.5).then_inc(power_set.sem, 1)
            pool.wait_ge(power_set.sem, power_set.at(0))

            def exponent(ap):
                return power[:, 0:ap.shape[1]]

            def root_mean(chain, ap, n, eps):
                carrier.take()
                chain.step(nc.gpsimd.tensor_scalar(ap, ap, 1.0 / n, eps, ALU.mult, ALU.add))
                return nc.gpsimd.tensor_tensor(ap, ap, exponent(ap), ALU.pow)

            def deviation(chain, norm, mv, s):
                pool.wait_ge(norm[0].sem, norm[0].at(s))
                carrier.take()
                chain.step(nc.gpsimd.tensor_scalar(mv[:, :, 1:2], mv[:, :, 1:2], 1e-5, None, ALU.add))
                nc.gpsimd.tensor_tensor(mv[:, :, 1:2], mv[:, :, 1:2], power[:, 0:NT].unsqueeze(2), ALU.pow
                                        ).then_inc(norm[1].sem, 1)

            def f1(s):
                pa_.start(s)
                pool.wait_ge(bc_squares.sem, bc_squares.at(s))
                root_mean(pa_, ssq[:, :, :].rearrange("p t m -> p (t m)"), N, 1e-6).then_inc(bc_rms.sem, 1)

            def a5(s):
                pa_.go_on(s)
                pool.wait_ge(yss_ready.sem, yss_ready.at(s))
                root_mean(pa_, yss[:, :], DI, 1e-6).then_inc(y_rms.sem, 1)

            def a6(s):
                deviation(pa_, norm1, mv1, s)
                pa_.end()

            def b2(s):
                pb_.start(s)
                pool.wait_ge(norm2[0].sem, norm2[0].at(s))
                carrier.take()
                nc.gpsimd.tensor_scalar(scales[:, 0:NT], mv2[:, :, 1], 1.0, LN_EPS, ALU.mult, ALU.add)
                pb_.step(nc.gpsimd.tensor_scalar(scales[:, NT:2 * NT], mv2[:, :, 1], 1.0 + RMS_EPS, RMS_EPS * LN_EPS,
                                                 ALU.mult, ALU.add))
                nc.gpsimd.tensor_tensor(scales[:, :], scales[:, :], power[:, :], ALU.pow).then_inc(norm2[1].sem, 1)

            def b3(s):
                pool.wait_ge(qk_ss_ready.sem, qk_ss_ready.at(s))
                pb_.step(root_mean(pb_, qk_ss[:, :, :].rearrange("p t m -> p (t m)"), D, RMS_EPS))
                carrier.take()
                nc.gpsimd.tensor_scalar(qk_ss[:, :, 0:1], qk_ss[:, :, 0:1], -1.0, None, ALU.mult
                                        ).then_inc(qk_rms_ready.sem, 1)

            def a2(s):
                pool.wait_ge(g_ready.sem, g_ready.at(s))
                pool.wait_ge(xs_ready.sem, xs_ready.at(s))
                nc.gpsimd.tensor_tensor(heads(xg[:, :, :]), heads(xs[:, :, :]), spread(g[:, :, :], 3, HD), ALU.mult
                                        ).then_inc(xg_ready.sem, 1)
                pool.wait_ge(coef_ready.sem, coef_ready.at(s))
                nc.gpsimd.tensor_tensor(heads(y[:, :, :]), heads(xs[:, :, :]), spread(coef[:, :, :], 3, HD), ALU.mult
                                        ).then_inc(y_added.sem, 1)

            def a3_late(s):
                pool.wait_ge(cb_copied.sem, cb_copied.at(s))
                for k0, k1 in ((0, 2), (2, LV)):
                    for t in range(NT):
                        nc.gpsimd.tensor_tensor(masked[:, t, k0:k1, :], spread(cb_all[:, t, :], 1, k1 - k0),
                                                const[:, MASK0 + k0:MASK0 + k1, :], ALU.mult
                                                ).then_inc(masked_ready.sem, 1)

            def a4(s, k):
                first = 0 if k < LV else 1
                pool.wait_ge(v_scaled.sem, v_scaled.at(s, k + 1))
                pool.wait_ge(y_added.sem, y_added.at(s, k + 1))
                nc.gpsimd.tensor_tensor(y[:, first:NT, :], y[:, first:NT, :], v[:, k % 2, first:NT, :], ALU.add
                                        ).then_inc(y_added.sem, 1)

            def b6(s, t):
                if t < NT - 1:
                    return
                deviation(pb_, norm3, mv2, s)
                pb_.end()

            def d8(s):
                if isinstance(s, int) and s == 0:
                    pool.wait_ge(padding_stored.sem, padding_stored.at(0))
                pool.wait_ge(meta_ready.sem, meta_ready.at(s))
                carrier.take()
                for t in range(NT):
                    for j in range(TOPK):
                        nc.gpsimd.indirect_dma_start(
                            out=meta_dram, out_offset=bass.IndirectOffsetOnAxis(ap=slot[:, t, j:j + 1], axis=0),
                            in_=meta[:, t, j, :], in_offset=None).then_inc(meta_stored.sem, 16)

            run_skewed(pool, nseq, {"F1": f1, "A2": a2, "A3L": a3_late, "A4": a4, "A5": a5, "A6": a6, "B2": b2, "B3": b3,
                                    "B6": b6, "D8": d8})
            pool.wait_ge(meta_stored.sem, meta_stored.at(nseq - 1))

        @block.vector
        def _(dve):
            vec = nc.vector
            carrier = Carrier(dve, dve_waited)
            ca = Chain(dve, dve_a.sem, DVE_A)
            cb_ = Chain(dve, dve_b.sem, DVE_B)

            dve.wait_ge(setup_loaded.sem, setup_loaded.at(0))
            dve.wait_ge(a_exp.sem, a_exp.at(0))
            vec.tensor_scalar(neg_a[:, :], neg_a[:, :], -1.0, None, ALU.mult)
            vec.tensor_scalar(bc_bias[:, 1, :], bc_bias[:, 1, :], float(N) ** -0.5, None, ALU.mult)
            vec.memset(base[:, :], 0.0)
            vec.memset(meta[:, :, :, :], 0)
            vec.tensor_copy(dst[:, :, :].rearrange("p t j -> p (t j)"), small[:, SM_DST:SM_TRI])
            for t in range(NT):
                last = vec.tensor_scalar(tok[:, t:t + 1], small[:, SM_P:SM_P + 1], float(t * P), None, ALU.add)
            last.then_inc(setup_done.sem, 1)
            dve.wait_ge(setup_done.sem, setup_done.at(0))

            def b_and_c():
                return rest[:, :, 0:2 * N].rearrange("p t (m n) -> p t m n", n=N)

            def f1(s):
                ca.start(s)
                dve.wait_ge(rest_copied.sem, rest_copied.at(s))
                o = 2 * N
                ca.step(vec.tensor_tensor(vl[:, :, 0:H], rest[:, :, o:o + H], spread(dt_bias[:, :], 1, NT), ALU.add))
                vec.tensor_scalar(vl[:, :, H:2 * H], rest[:, :, o + H:o + 2 * H], -1.0, None, ALU.mult)
                vec.tensor_scalar(vl[:, :, 0:H], vl[:, :, 0:H], 0.0, -9.3, ALU.min, ALU.max).then_inc(v_ready.sem, 1)
                bc = b_and_c()
                ca.step(vec.tensor_tensor(bct[:, :, :, :], bc, bc, ALU.mult))
                vec.tensor_reduce(ssq[:, :, :], bct[:, :, :, :], AX_X, ALU.add).then_inc(bc_squares.sem, 1)

            def f2(s):
                dve.wait_ge(eu_ready.sem, eu_ready.at(s))
                vec.tensor_scalar(vl[:, :, :], eu[:, :, :], 1.0, None, ALU.add).then_inc(w_ready.sem, 1)

            def f4(s, k):
                if k == 0:
                    dve.wait_ge(bc_rms.sem, bc_rms.at(s))
                    ca.step(vec.tensor_tensor(bcn[:, :, :, :], b_and_c(), spread(ssq[:, :, :], 3, N), ALU.mult))
                    ca.step(vec.tensor_tensor(bcn[:, :, :, :], bcn[:, :, :, :], spread(bc_bias[:, :, :], 1, NT),
                                              ALU.mult))
                    dve.wait_ge(w_ready.sem, w_ready.at(s))
                    vec.tensor_scalar(rec[:, :, 0:H], vl[:, :, 0:H], -1.0, None, ALU.add)
                    ca.step(vec.tensor_copy(rec[:, :, H:2 * H], vl[:, :, H:2 * H]))
                    return
                ca.go_on(s)
                if k == 1:
                    ca.step(vec.reciprocal(rec[:, :, :], rec[:, :, :]))
                    return
                ca.step(vec.tensor_tensor(dt[:, :, :], eu[:, :, 0:H], rec[:, :, 0:H], ALU.mult))
                dve.wait_ge(ln_ready.sem, ln_ready.at(s))
                ca.step(vec.tensor_tensor(dt[:, :, :], dt[:, :, :], lnw[:, :, :], ALU.mult))
                ca.step(vec.tensor_scalar(dt[:, :, :], dt[:, :, :], DT_MIN, DT_MAX, ALU.max, ALU.min))
                vec.tensor_tensor(d_a[:, :, :], dt[:, :, :], spread(neg_a[:, :], 1, NT), ALU.mult)
                vec.tensor_tensor(ld[:, :, :], dt[:, :, :], rec[:, :, H:2 * H], ALU.mult)
                ca.step(vec.tensor_reduce(dtm[:, :], dt[:, :, :], AX_X, ALU.add))
                vec.tensor_tensor(q[:, :, :], dt[:, :, :], ld[:, :, :], ALU.subtract)
                for t in range(NT):
                    last = vec.tensor_scalar(dth[:, t, :], rest[:, t, REST - N // 2:REST], dtm[:, t:t + 1], 1.0 / H,
                                             ALU.mult, ALU.mult)
                last.then_inc(steps_ready.sem, 1)

            def a2(s):
                ca.go_on(s)
                dve.wait_ge(shifted.sem, shifted.at(s))
                cum = pa[:, 2, 2 * H:2 * H + N].rearrange("p (t n) -> p t n", t=NT)
                vec.tensor_scalar(ang[:, :, 0, :], cum, float(np.pi / 2), None, ALU.add)
                ca.step(vec.tensor_copy(ang[:, :, 1, :], cum))
                ca.step(vec.tensor_scalar(turns[:, :, :, :], ang[:, :, :, :], float(0.5 / np.pi), MAGIC,
                                          ALU.mult, ALU.add))
                ca.step(vec.tensor_scalar(turns[:, :, :, :], turns[:, :, :, :], MAGIC, None, ALU.subtract))
                flat = "p t c n -> p (t c n)"
                an, tu = ang[:, :, :, :].rearrange(flat), turns[:, :, :, :].rearrange(flat)
                ca.step(vec.scalar_tensor_tensor(an, tu, -TWO_PI_HI, an, ALU.mult, ALU.add))
                ca.step(vec.scalar_tensor_tensor(an, tu, -TWO_PI_LO, an, ALU.mult, ALU.add))
                vec.tensor_scalar(an, an, 3.1415925, -3.1415925, ALU.min, ALU.max).then_inc(ang_ready.sem, 1)
                vec.tensor_tensor(g[:, :, :], ld[:, :, :], pa[:, 2, 0:2 * H].rearrange("p (t h) -> p t h", t=NT),
                                  ALU.add).then_inc(g_ready.sem, 1)
                dve.wait_ge(sin_ready.sem, sin_ready.at(s))
                half = N // 2

                def halves(ap):
                    return ap.rearrange("p t m (f n) -> p t (m f) n", n=half)

                vec.tensor_tensor(halves(bct[:, :, :, :]), halves(bcn[:, :, :, :]), spread(cs[:, :, 0, :], 2, 4), ALU.mult)
                ca.step(vec.tensor_tensor(halves(bcu[:, :, :, :]), halves(bcn[:, :, :, :]), spread(cs[:, :, 1, :], 2, 4),
                                          ALU.mult))
                vec.tensor_tensor(bcr[:, :, :, 0:half], bct[:, :, :, 0:half], bcu[:, :, :, half:N], ALU.add)
                vec.tensor_tensor(bcr[:, :, :, half:N], bct[:, :, :, half:N], bcu[:, :, :, 0:half], ALU.subtract
                                  ).then_inc(roped.sem, 1)
                dve.wait_ge(roped.sem, roped.at(s))
                ca.step(vec.tensor_tensor(bct[:, :, 0, :], bcr[:, :, 0, :], bcr[:, :, 1, :], ALU.mult))
                ca.step(vec.tensor_reduce(cb[:, :], bct[:, :, 0, :], AX_X, ALU.add))
                vec.tensor_tensor(coef[:, :, :], ld[:, :, :], spread(cb[:, :], 2, H), ALU.mult
                                  ).then_inc(coef_ready.sem, 1)

            def a2_late(s):
                dve.wait_ge(decay_ready.sem, decay_ready.at(s))
                dve.wait_ge(xg_ready.sem, xg_ready.at(s))

            def decayed(s, k):
                tiles = NT if k < LV else 1
                if k >= US:
                    dve.wait_ge(level_done.sem, level_done.at(s, k - US + 1))
                vec.tensor_tensor(heads(u[:, k % US, 0:tiles, :]), heads(xg[:, 0:tiles, :]),
                                  spread(decay[:, k, 0:tiles, :], 3, HD), ALU.mult).then_inc(u_ready.sem, 1)

            def a4(s, k):
                first = 0 if k < LV else 1
                dve.wait_ge(level_done.sem, level_done.at(s, k + 1))
                if k >= 2:
                    dve.wait_ge(y_added.sem, y_added.at(s, k))
                b = 2 * (k % 2)
                vec.tensor_tensor(heads(v[:, k % 2, first:NT, :]), heads(pa[:, b + first:b + NT, :]),
                                  spread(decay[:, k, first:NT, :], 3, HD), ALU.mult).then_inc(v_scaled.sem, 1)

            def a5(s):
                ca.go_on(s)
                dve.wait_ge(y_rms.sem, y_rms.at(s))
                for t in range(NT):
                    vec.scalar_tensor_tensor(y[:, t, :], y[:, t, :], yss[:, t:t + 1], zs[:, t, :], ALU.mult, ALU.mult
                                             ).then_inc(yn_ready.sem, 1)

            def a6(s):
                ca.go_on(s)
                dve.wait_ge(out_projected.sem, out_projected.at(s))
                dve.wait_ge(x_row_in.sem, x_row_in.at(s))
                ca.step(vec.tensor_tensor(r1[:, :, :], x_row[:, :, :], pa[:, 2, :].rearrange("p (t d) -> p t d", t=NT),
                                          ALU.add))
                if later(s):
                    dve.wait_ge(x2_ready.sem, x2_ready.before(s))
                layer_norm(ca, s, r1, st1, mv1, norm1, x1, x1_ready)
                ca.end()
                if isinstance(s, int) and s == 0:
                    dve.wait_ge(weights_loaded.sem, weights_loaded.at(0))
                    for w in (w_gate, w_up):
                        vec.tensor_scalar(w[:, :, :], w[:, :, :].bitcast(I32), -128.0, None, ALU.add
                                          ).then_inc(dequantised.sem, 1)
                    vec.tensor_scalar(w_down[:, 0:FJ - 1, :], w_down[:, 0:FJ - 1, :].bitcast(I32), -128.0, None, ALU.add
                                      ).then_inc(dequantised.sem, 1)
                    r = FH - (FJ - 1) * P
                    vec.tensor_scalar(w_down[0:r, FJ - 1, :], w_down[0:r, FJ - 1, :].bitcast(I32), -128.0, None, ALU.add
                                      ).then_inc(dequantised.sem, 1)
                    dve.wait_ge(dequantised.sem, dequantised.at(0, 4))
                    vec.tensor_tensor(w_down[:, 0:FJ - 1, :], w_down[:, 0:FJ - 1, :], spread(s_down[:, :], 1, FJ - 1),
                                      ALU.mult).then_inc(dequantised.sem, 1)
                    vec.tensor_tensor(w_down[0:r, FJ - 1, :], w_down[0:r, FJ - 1, :], s_down[0:r, :],
                                      ALU.mult).then_inc(dequantised.sem, 1)

            def statistics(chain, src, stats, mv, norm):
                for t in range(NT):
                    last = vec.bn_stats(stats[:, t, :], src[:, t, :])
                chain.step(last)
                carrier.take()
                for t in range(NT):
                    last = vec.bn_aggr(mv[:, t, :], stats[:, t, :])
                last.then_inc(norm[0].sem, 1)

            def layer_norm(chain, s, src, stats, mv, norm, to, done):
                statistics(chain, src, stats, mv, norm)
                dve.wait_ge(norm[1].sem, norm[1].at(s))
                for t in range(NT):
                    vec.tensor_scalar(to[:, t, :], src[:, t, :], mv[:, t, 0:1], mv[:, t, 1:2], ALU.subtract, ALU.mult
                                      ).then_inc(done.sem, 1)

            def b1(s, j):
                rows = min(P, FH - j * P)
                dve.wait_ge(ffn_silu.sem, ffn_silu.at(s, j + 1))
                vec.scalar_tensor_tensor(hT[0:rows, j, :], pb[0:rows, 1 + j % 2, T:2 * T], s_gu[0:rows, 1, j:j + 1],
                                         sg[0:rows, j % 2, :], ALU.mult, ALU.mult).then_inc(ffn_h.sem, 1)

            def b2(s):
                cb_.start(s)
                dve.wait_ge(ffn_out.sem, ffn_out.at(s))
                dve.wait_ge(x1_ready.sem, x1_ready.at(s))
                cb_.step(vec.tensor_tensor(r2[:, :, :], pb[:, 3, :].rearrange("p (t d) -> p t d", t=NT), x1[:, :, :],
                                           ALU.add))
                statistics(cb_, r2, st2, mv2, norm2)

            def b2_late(s):
                dve.wait_ge(norm2[1].sem, norm2[1].at(s))
                for o, to, done in ((NT, x2n, x2n_ready), (0, x2, x2_ready)):
                    for t in range(NT):
                        vec.tensor_scalar(to[:, t, :], r2[:, t, :], mv2[:, t, 0:1], scales[:, o + t:o + t + 1],
                                          ALU.subtract, ALU.mult).then_inc(done.sem, 1)

            def b3(s):
                dve.wait_ge(v_projected.sem, v_projected.at(s))
                for t in range(NT):
                    dve.wait_ge(k_exp.sem, k_exp.at(s, t + 1))
                    vec.tensor_tensor(wv[:, t, 1, :], wv[:, t, 0, :], pb[:, 3, t * D:(t + 1) * D], ALU.mult
                                      ).then_inc(wv_ready.sem, 1)

            def b4(s):
                dve.wait_ge(q_exp.sem, q_exp.at(s))
                cb_.step(vec.tensor_scalar(eq[:, :, :], eq[:, :, :], 1.0, None, ALU.add))
                dve.wait_ge(cumulated.sem, cumulated.at(s))
                cb_.step(vec.scalar_tensor_tensor(den[:, :, :], pb[:, 1:1 + NT, 0:D], 1e-6, eq[:, :, :],
                                                  ALU.add, ALU.mult))
                cb_.step(vec.reciprocal(den[:, :, :], den[:, :, :]))
                vec.tensor_tensor(yc[:, :, :], den[:, :, :], pb[:, 1:1 + NT, D:2 * D], ALU.mult
                                  ).then_inc(yc_ready.sem, 1)

            def b5(s, j):
                dve.wait_ge(sw_silu.sem, sw_silu.at(s, j + 1))
                vec.tensor_tensor(hT[:, j, :], pb[:, 1 + j % 2, T:2 * T], sg[:, j % 2, :], ALU.mult
                                  ).then_inc(sw_h.sem, 1)

            def b6(s, t):
                if t < NT - 1:
                    return
                dve.wait_ge(sw_out.sem, sw_out.at(s))
                cb_.step(vec.scalar_tensor_tensor(r2[:, :, :], x2[:, :, :], 2.0,
                                                  pb[:, 3, :].rearrange("p (t d) -> p t d", t=NT), ALU.mult, ALU.add))
                if later(s):
                    dve.wait_ge(x3_stored.sem, x3_stored.before(s))
                layer_norm(cb_, s, r2, st2, mv2, norm3, x3, x3_ready)

            def c7_late(s):
                cb_.go_on(s)
                dve.wait_ge(logits_copied.sem, logits_copied.at(s))
                carrier.take()
                for t in range(NT):
                    last = vec.max(top[:, t, :], logits[:, t, :])
                cb_.step(last)
                carrier.take()
                for t in range(NT):
                    vec.max_index(topi[:, t, :], top[:, t, :], logits[:, t, :])
                vec.tensor_tensor(ez[:, :, :], top[:, :, 0:TOPK], top[:, :, 0:1].broadcast_to([P, NT, TOPK]),
                                  ALU.subtract).then_inc(gap_ready.sem, 1)
                dve.wait_ge(gap_ready.sem, gap_ready.at(s))
                cb_.step(vec.tensor_copy(topf[:, :, :], topi[:, :, 0:TOPK]))
                for t in range(NT):
                    last = vec.tensor_tensor(hot[:, t, :, :], spread(small[:, SM_E:SM_DST], 1, TOPK),
                                             spread(topf[:, t, :], 2, NE), ALU.is_equal)
                cb_.step(last)
                vec.tensor_reduce(chosen[:, :, :], hot[:, :, :, :].rearrange("p t j e -> p t e j"), AX_X, ALU.add
                                  ).then_inc(chosen_ready.sem, 1)

            def c8(s):
                cb_.go_on(s)
                dve.wait_ge(top_exp.sem, top_exp.at(s))
                cb_.step(vec.tensor_reduce(esum[:, :], ez[:, :, :], AX_X, ALU.add))
                cb_.step(vec.reciprocal(esum[:, :], esum[:, :]))
                if later(s):
                    dve.wait_ge(meta_stored.sem, meta_stored.before(s))
                vec.tensor_tensor(meta[:, :, :, 2].bitcast(F32), ez[:, :, :], spread(esum[:, :], 2, TOPK), ALU.mult)
                vec.tensor_copy(meta[:, :, :, 0], dst[:, :, :])
                cb_.step(vec.tensor_copy(meta[:, :, :, 1], spread(tok[:, :], 2, TOPK)))
                vec.tensor_scalar(dst[:, :, :], dst[:, :, :], float(T * TOPK), None, ALU.add)
                vec.tensor_scalar(tok[:, :], tok[:, :], float(T), None, ALU.add)
                dve.wait_ge(counted.sem, counted.at(s))
                cb_.step(vec.tensor_tensor(pos[:, :, :], pb[:, 3, 0:NT * NE].rearrange("p (t e) -> p t e", t=NT),
                                           spread(base[:, :], 1, NT), ALU.add))
                vec.tensor_tensor(base[:, :], base[:, :], pb[:, 3, NT * NE:(NT + 1) * NE], ALU.add)
                for t in range(NT):
                    last = vec.tensor_tensor(hot_pos[:, t, :, :], hot[:, t, :, :], spread(pos[:, t, :], 1, TOPK), ALU.mult)
                cb_.step(last)
                cb_.step(vec.tensor_reduce(slot_f[:, :, :], hot_pos[:, :, :, :], AX_X, ALU.add))
                flat = "p t j -> p (t j)"
                vec.scalar_tensor_tensor(slot[:, :, :].rearrange(flat), topf[:, :, :].rearrange(flat), float(cap),
                                         slot_f[:, :, :].rearrange(flat), ALU.mult, ALU.add
                                         ).then_inc(meta_ready.sem, 1)
                cb_.end()

            run_skewed(dve, nseq, {"F1": f1, "F2": f2, "F4": f4, "A2": a2, "A2L": a2_late, "AU": decayed, "A4": a4, "A5": a5,
                                   "A6": a6, "B1": b1, "B2": b2, "B2L": b2_late, "B3": b3, "B4": b4, "B5": b5,
                                   "B6": b6, "C7L": c7_late, "C8": c8})


def heads(ap):
    return ap.rearrange("p t (h d) -> p t h d", d=HD)


def experts_block(nc, ins, ntok, cap, ntile, ident, small, base, meta_dram, x3_dram, yk_dram):
    pieces = 2 * DC + 2
    XS = UN // 2
    SS = 4
    with ExitStack() as ctx:
        def sb(name, shape, dt=F32):
            return ctx.enter_context(nc.sbuf_tensor(name, shape, dt))

        def sig(name, per):
            return Signal(ctx.enter_context(nc.semaphore(name)), per)

        w_ug = sb("w_ug", [P, NE, 2, DC, 2 * EH], BF16)
        w_dn = sb("w_dn", [EC, NE, 2, EJ, D], BF16)
        stage = sb("stage", [P, SS, EJ // 2 * D])
        tiles_of = sb("tiles_of", [P, NE])
        upto = sb("upto", [P, NE])
        table = sb("table", [1, 2, ntile], I32)
        meta = sb("meta_in", [P, UN, 4], U32)
        xin = sb("xin", [P, XS, D])
        xh = sb("xh", [P, 2, 2, DC, P], BF16)
        gate_hid = sb("gate_hid", [P, 3, EH])
        gate, hid = gate_hid[:, 0, :], gate_hid[:, 1:3, :]
        early_hid = gate_hid[0:1, :, :].rearrange("p a b -> p (a b)")
        passed = early_hid.bitcast(BF16)[:, 0:ntile * NE].rearrange("p (i e) -> p i e", e=NE)
        tile_o = early_hid[:, ntile * NE // 2:ntile * NE // 2 + ntile]
        early_x = xh[:, :, :, :, :].rearrange("p b h c l -> p (b h c l)").bitcast(F32)
        tri = early_x[:, 0:NE * NE].rearrange("p (a b) -> p a b", a=NE)
        tile_e = early_x[0:1, NE * NE:NE * NE + ntile]
        hh = sb("hh", [EC, 2, 2, EJ, P], BF16)
        yo = sb("yo", [P, 2, D])

        pu = ctx.enter_context(nc.psum_tensor("pu", [P, 4, 512], F32))
        ph = ctx.enter_context(nc.psum_tensor("ph", [P, 2, 512], F32))
        px = ctx.enter_context(nc.psum_tensor("px", [P, 512], F32))
        py = ctx.enter_context(nc.psum_tensor("py", [P, 512], F32))
        ident = ident[:, :]

        piece_in = [sig(f"piece_in{n}", 16) for n in range(SS)]
        high_done = sig("high_done", pieces)
        weights_ready = sig("weights_ready", pieces)
        list_step = sig("list_step", 12)
        table_ready = sig("table_ready", 1)
        pool_waited, sp_waited = (ctx.enter_context(nc.semaphore(f"{n}_waited_e")) for n in ("pool", "sp"))
        meta_in = [sig(f"meta_in{n}", 16) for n in range(UN)]
        x_in = [sig(f"x_in{n}", 16) for n in range(XS)]
        x_transposed = sig("x_transposed", 1)
        x_high = sig("x_high", 1)
        x_split = sig("x_split", 1)
        ug_done = sig("ug_done", 1)
        gate_ready = sig("gate_ready", 1)
        hid_ready = sig("hid_ready", 1)
        h_transposed = sig("h_transposed", 1)
        h_high = sig("h_high", 1)
        h_split = sig("h_split", 1)
        down_done = sig("down_done", 1)
        y_ready = sig("y_ready", 1)
        y_stored = [sig(f"y_stored{n}", 16) for n in range(2)]

        def piece_views(e, k):
            if k < 2 * DC:
                return P, EH, lambda part: w_ug[:, e, part, k // 2, k % 2 * EH:(k % 2 + 1) * EH]
            j = (k - 2 * DC) * EJ // 2
            return EC, EJ // 2 * D, lambda part: w_dn[:, e, part, j:j + EJ // 2, :].rearrange("p j d -> p (j d)")

        def steps(eng, run, first, last):
            lo, hi = NE // UN, ntile // UN - 1
            for i in range(first, UN * lo):
                run(i // UN, i % UN)
            if hi > lo:
                with eng.Fori(lo, hi) as r:
                    for m in range(UN):
                        run(r, m)
            for i in range(UN * max(hi, lo), last):
                run(i // UN, i % UN)

        def parts(r, m, shift, **runs):
            r, m = r + (m + shift) // UN, (m + shift) % UN
            if not isinstance(r, int) or 0 <= UN * r + m < ntile:
                for run in runs.values():
                    run(r, m)

        def pieces_of(r, m, run, ahead=0):
            if isinstance(r, int):
                for n in range(pieces * (UN * r + m + 1) + ahead, pieces * (UN * r + m + 2) + ahead):
                    if n < NE * pieces:
                        run(n // pieces, n % pieces)

        block = ctx.enter_context(nc.Block())

        @block.sync
        def _(sp):
            def load_piece(e, k):
                n = e * pieces + k
                rows, width, _ = piece_views(e, k)
                if n >= SS:
                    sp.wait_ge(weights_ready.sem, n - SS + 1)
                to = stage[0:rows, n % SS, 0:width]
                if k < 2 * DC:
                    src = ins["w_ug"][e, k // 2 * P:(k // 2 + 1) * P, k % 2 * EH:(k % 2 + 1) * EH]
                else:
                    to = to.rearrange("p (j d) -> p j d", d=D)
                    src = ins["w_dn"][e].rearrange("(j p) d -> p j d", p=EC)[
                        :, (k - 2 * DC) * EJ // 2:(k - 2 * DC + 1) * EJ // 2, :]
                sp.dma_start(to, src).then_inc(piece_in[n % SS].sem, 16)

            carrier = Carrier(sp, sp_waited)

            def load_meta(r, m):
                i = UN * r + m
                if later(i, UN):
                    sp.wait_ge(y_stored[m % 2].sem, y_stored[m % 2].at(UN // 2 * (r - 1) + m // 2))
                carrier.take()
                row = sp.value_load(table[0:1, 1, bass.ds(i, 1)], min_val=0, max_val=NE * cap)
                sp.dma_start(meta[:, m, :], meta_dram[bass.ds(row, P), :]).then_inc(meta_in[m].sem, 16)

            for n in range(SS):
                load_piece(n // pieces, n % pieces)
            sp.wait_ge(table_ready.sem, table_ready.at(0))
            for i in range(3):
                load_meta(0, i)

            def step(r, m):
                parts(r, m, 4, run=load_meta)
                pieces_of(r, m, load_piece, SS)

            steps(sp, step, -1, ntile)

        @block.tensor
        def _(pe):
            mm = nc.tensor.matmul

            def transpose_x(r, m):
                i = UN * r + m
                pe.wait_ge(x_in[m % XS].sem, x_in[m % XS].at(2 * r + m // XS))
                if later(i):
                    pe.wait_ge(x_split.sem, x_split.before(i))
                for c in range(DC):
                    last = nc.tensor.transpose(px[:, c * P:(c + 1) * P], xin[:, m % XS, c * P:(c + 1) * P], ident)
                last.then_inc(x_transposed.sem, 1)

            def up_gate(r, m):
                i = UN * r + m
                b = m % 2
                e = pe.value_load(table[0:1, 0, bass.ds(i, 1)], min_val=0, max_val=NE - 1)
                pe.wait_ge(x_split.sem, x_split.at(i))
                pe.wait_ge(weights_ready.sem, (e + 1) * pieces)
                if later(i, 2):
                    pe.wait_ge(hid_ready.sem, hid_ready.at(i - 2))
                for w in range(2):
                    n = 0
                    for c in range(DC):
                        for xp, wp in ((0, 0), (0, 1), (1, 0)):
                            last = mm(pu[:, 2 * b + w, 0:EH], xh[:, b, xp, c, :],
                                      w_ug[:, bass.ds(e, 1), wp, c, w * EH:(w + 1) * EH],
                                      start=n == 0, stop=n == 3 * DC - 1)
                            n += 1
                last.then_inc(ug_done.sem, 1)

            def transpose_h(r, m):
                i = UN * r + m
                b = m % 2
                pe.wait_ge(hid_ready.sem, hid_ready.at(i))
                if later(i, 2):
                    pe.wait_ge(h_split.sem, h_split.at(i - 2))
                for j in range(EJ):
                    last = nc.tensor.transpose(ph[0:EC, b, j * P:(j + 1) * P], hid[:, b, j * EC:(j + 1) * EC], ident)
                last.then_inc(h_transposed.sem, 1)

            def down(r, m):
                i = UN * r + m
                b = m % 2
                e = pe.value_load(table[0:1, 0, bass.ds(i, 1)], min_val=0, max_val=NE - 1)
                pe.wait_ge(h_split.sem, h_split.at(i))
                if later(i):
                    pe.wait_ge(y_ready.sem, y_ready.before(i))
                n = 0
                for j in range(EJ):
                    for hp, wp in ((0, 0), (0, 1), (1, 0)):
                        last = mm(py[:, 0:D], hh[:, b, hp, j, :], w_dn[:, bass.ds(e, 1), wp, j, :],
                                  start=n == 0, stop=n == 3 * EJ - 1)
                        n += 1
                last.then_inc(down_done.sem, 1)

            pe.wait_ge(table_ready.sem, table_ready.at(0))

            def step(r, m):
                parts(r, m, 0, run=up_gate)
                parts(r, m, -1, run=transpose_h)
                parts(r, m, 1, run=transpose_x)
                parts(r, m, -2, run=down)

            steps(pe, step, -1, ntile + 2)

        @block.scalar
        def _(act):
            act_f = nc.scalar.activation

            def high(e, k):
                n = e * pieces + k
                rows, width, part = piece_views(e, k)
                act.wait_ge(piece_in[n % SS].sem, piece_in[n % SS].at(n // SS))
                act_f(part(0), stage[0:rows, n % SS, 0:width], ACT.Copy).then_inc(high_done.sem, 1)

            def x_part(r, m):
                i = UN * r + m
                act.wait_ge(x_transposed.sem, x_transposed.at(i))
                if later(i, 2):
                    act.wait_ge(ug_done.sem, ug_done.at(i - 2))
                act_f(xh[:, m % 2, 0, :, :].rearrange("p c l -> p (c l)"), px[:, 0:D], ACT.Copy
                      ).then_inc(x_high.sem, 1)

            def gate_part(r, m):
                i = UN * r + m
                act.wait_ge(ug_done.sem, ug_done.at(i))
                if later(i):
                    act.wait_ge(hid_ready.sem, hid_ready.before(i))
                act_f(gate, pu[:, 2 * (m % 2) + 1, 0:EH], ACT.Silu).then_inc(gate_ready.sem, 1)

            def h_part(r, m):
                i = UN * r + m
                act.wait_ge(h_transposed.sem, h_transposed.at(i))
                if later(i, 2):
                    act.wait_ge(down_done.sem, down_done.at(i - 2))
                act_f(hh[:, m % 2, 0, :, :].rearrange("p j l -> p (j l)"), ph[0:EC, m % 2, :], ACT.Copy
                      ).then_inc(h_high.sem, 1)

            def step(r, m):
                pieces_of(r, m, high)
                parts(r, m, -1, run=h_part)
                parts(r, m, 1, run=x_part)
                parts(r, m, 0, run=gate_part)

            steps(act, step, -1, ntile + 2)

        @block.vector
        def _(dve):
            vec = nc.vector
            chain = Chain(dve, list_step.sem, list_step.per)
            chain.step(vec.tensor_scalar(tiles_of[:, :], base[:, :], 1.0 / P, (P - 1) / P - 0.5 + 0.5 / P,
                                         ALU.mult, ALU.add))
            chain.step(vec.tensor_scalar(tiles_of[:, :], tiles_of[:, :], MAGIC, None, ALU.add))
            chain.step(vec.tensor_scalar(tiles_of[:, :], tiles_of[:, :], MAGIC, 1.0, ALU.subtract, ALU.max))
            chain.step(vec.tensor_tensor(tri[:, :, :], small[:, SM_TRI:SM_I].rearrange("p (a b) -> p a b", a=NE),
                                         spread(tiles_of[:, :], 1, NE), ALU.mult))
            chain.step(vec.tensor_reduce(upto[:, :], tri[:, :, :], AX_X, ALU.add))
            number = small[0:1, SM_I:SM_I + ntile]
            chain.step(vec.tensor_tensor(passed[:, :, :], spread(upto[0:1, :], 1, ntile), spread(number, 2, NE), ALU.is_le))
            chain.step(vec.tensor_reduce(tile_e[:, :], passed[:, :, :], AX_X, ALU.add))
            chain.step(vec.tensor_tensor(passed[:, :, :], passed[:, :, :], spread(tiles_of[0:1, :], 1, ntile), ALU.mult))
            chain.step(vec.tensor_reduce(tile_o[:, :], passed[:, :, :], AX_X, ALU.add))
            chain.step(vec.tensor_tensor(tile_o[:, :], number, tile_o[:, :], ALU.subtract))
            chain.step(vec.tensor_scalar(tile_o[:, :], tile_o[:, :], float(P), None, ALU.mult))
            chain.step(vec.scalar_tensor_tensor(tile_o[:, :], tile_e[:, :], float(cap), tile_o[:, :], ALU.mult, ALU.add))
            chain.end()
            vec.tensor_scalar(table[:, 0, :], tile_e[:, :], float(NE - 1), None, ALU.min)
            vec.tensor_scalar(table[:, 1, :], tile_o[:, :], float(NE * cap), None, ALU.min).then_inc(table_ready.sem, 1)

            def low(e, k):
                n = e * pieces + k
                rows, width, part = piece_views(e, k)
                dve.wait_ge(high_done.sem, n + 1)
                vec.tensor_tensor(part(1), stage[0:rows, n % SS, 0:width], part(0), ALU.subtract
                                  ).then_inc(weights_ready.sem, 1)

            def x_part(r, m):
                i = UN * r + m
                dve.wait_ge(x_high.sem, x_high.at(i))
                vec.tensor_tensor(xh[:, m % 2, 1, :, :].rearrange("p c l -> p (c l)"), px[:, 0:D],
                                  xh[:, m % 2, 0, :, :].rearrange("p c l -> p (c l)"), ALU.subtract
                                  ).then_inc(x_split.sem, 1)

            def hidden(r, m):
                i = UN * r + m
                dve.wait_ge(gate_ready.sem, gate_ready.at(i))
                if later(i, 2):
                    dve.wait_ge(h_transposed.sem, h_transposed.at(i - 2))
                vec.tensor_tensor(hid[:, m % 2, :], pu[:, 2 * (m % 2), 0:EH], gate, ALU.mult
                                  ).then_inc(hid_ready.sem, 1)

            def h_part(r, m):
                i = UN * r + m
                dve.wait_ge(h_high.sem, h_high.at(i))
                vec.tensor_tensor(hh[:, m % 2, 1, :, :].rearrange("p j l -> p (j l)"), ph[0:EC, m % 2, :],
                                  hh[:, m % 2, 0, :, :].rearrange("p j l -> p (j l)"), ALU.subtract
                                  ).then_inc(h_split.sem, 1)

            def y_part(r, m):
                i = UN * r + m
                dve.wait_ge(down_done.sem, down_done.at(i))
                if later(i, 2):
                    dve.wait_ge(y_stored[m % 2].sem, y_stored[m % 2].at(UN // 2 * r + m // 2 - 1))
                vec.tensor_scalar(yo[:, m % 2, :], py[:, 0:D], meta[:, m, 2:3].bitcast(F32), None, ALU.mult
                                  ).then_inc(y_ready.sem, 1)

            def step(r, m):
                pieces_of(r, m, low)
                parts(r, m, -1, run=h_part)
                parts(r, m, 1, run=x_part)
                parts(r, m, 0, run=hidden)
                parts(r, m, -2, run=y_part)

            steps(dve, step, -1, ntile + 2)

        @block.gpsimd
        def _(pool):
            carrier = Carrier(pool, pool_waited)
            def gather(r, m):
                i = UN * r + m
                pool.wait_ge(meta_in[m].sem, meta_in[m].at(r))
                if later(i, XS):
                    pool.wait_ge(x_transposed.sem, x_transposed.at(i - XS))
                carrier.take()
                nc.gpsimd.indirect_dma_start(
                    out=xin[:, m % XS, :], out_offset=None, in_=x3_dram,
                    in_offset=bass.IndirectOffsetOnAxis(ap=meta[:, m, 1:2], axis=0)
                ).then_inc(x_in[m % XS].sem, 16)

            def scatter(r, m):
                i = UN * r + m
                pool.wait_ge(y_ready.sem, y_ready.at(i))
                carrier.take()
                nc.gpsimd.indirect_dma_start(
                    out=yk_dram, out_offset=bass.IndirectOffsetOnAxis(ap=meta[:, m, 0:1], axis=0),
                    in_=yo[:, m % 2, :], in_offset=None, bounds_check=ntok * TOPK - 1, oob_is_err=False
                ).then_inc(y_stored[m % 2].sem, 16)

            def step(r, m):
                parts(r, m, -3, run=scatter)
                parts(r, m, 3, run=gather)

            gather(0, 0)
            gather(0, 1)
            steps(pool, step, -1, ntile + 3)
            for n in range(2):
                pool.wait_ge(y_stored[n].sem, y_stored[n].at(ntile // 2 - 1))


def combine_block(nc, nseq, x3_dram, yk_dram, out):
    CS = 4 if nseq % 4 == 0 else 1
    with ExitStack() as ctx:
        def sb(name, shape, dt=F32):
            return ctx.enter_context(nc.sbuf_tensor(name, shape, dt))

        def sig(name, per):
            return Signal(ctx.enter_context(nc.semaphore(name)), per)

        rows = sb("rows", [P, CS, NT, TOPK * D])
        res = sb("res", [P, CS, NT, D])
        st = sb("st", [P, NT, 6])
        mv = sb("mv", [P, CS, NT, 2])
        fin = sb("fin", [P, CS, NT, D])
        loaded = [sig(f"loaded{n}", 32) for n in range(CS)]
        summed = sig("summed", 1)
        norm_step = sig("norm_step", 3)
        power = sb("power_c", [P, 1])
        pool_waited, dve_waited = (ctx.enter_context(nc.semaphore(f"{n}_waited_c")) for n in ("pool", "dve"))
        power_set = sig("power_set", 1)
        shifted = sig("shifted_c", 1)
        variance_ready = sig("variance_ready", 1)
        deviation_ready = sig("deviation_ready", 1)
        normed = sig("normed", 1)
        stored = [sig(f"stored{n}", 16) for n in range(CS)]
        block = ctx.enter_context(nc.Block())

        def sequences(eng, run):
            for i in range(min(2 * CS, nseq)):
                run(i, i % CS, i // CS)
            if nseq > 2 * CS:
                with eng.Fori(2, nseq // CS) as r:
                    for m in range(CS):
                        run(CS * r + m, m, r)

        @block.sync
        def _(sp):
            def load(i, m, r):
                if later(i, CS):
                    sp.wait_ge(normed.sem, normed.at(i - CS))
                sp.dma_start(rows[:, m, :, :], yk_dram.rearrange("(n k) d -> n (k d)", k=TOPK)[bass.ds(i * T, T), :]
                             .rearrange("(t p) d -> p t d", p=P)).then_inc(loaded[m].sem, 16)
                sp.dma_start(res[:, m, :, :], x3_dram[bass.ds(i * T, T), :].rearrange("(t p) d -> p t d", p=P)
                             ).then_inc(loaded[m].sem, 16)

            sequences(sp, load)

        @block.gpsimd
        def _(pool):
            carrier = Carrier(pool, pool_waited)
            nc.gpsimd.memset(power[:, :], -0.5).then_inc(power_set.sem, 1)
            pool.wait_ge(power_set.sem, power_set.at(0))

            def deviation(i, m, r):
                pool.wait_ge(variance_ready.sem, variance_ready.at(i))
                carrier.take()
                nc.gpsimd.tensor_scalar(mv[:, m, :, 1:2], mv[:, m, :, 1:2], LN_EPS, None, ALU.add
                                        ).then_inc(shifted.sem, 1)
                pool.wait_ge(shifted.sem, shifted.at(i))
                nc.gpsimd.tensor_tensor(mv[:, m, :, 1:2], mv[:, m, :, 1:2], spread(power[:, :], 1, NT), ALU.pow
                                        ).then_inc(deviation_ready.sem, 1)

            sequences(pool, deviation)

        @block.vector
        def _(dve):
            vec = nc.vector
            chain = Chain(dve, norm_step.sem, norm_step.per)
            carrier = Carrier(dve, dve_waited)

            def sums(i, m, r):
                chain.start(i)
                dve.wait_ge(loaded[m].sem, loaded[m].at(r))
                chain.step(vec.tensor_tensor(rows[:, m, :, 0:2 * D], rows[:, m, :, 0:2 * D], rows[:, m, :, 2 * D:4 * D],
                                             ALU.add))
                chain.step(vec.tensor_tensor(rows[:, m, :, 0:D], rows[:, m, :, 0:D], rows[:, m, :, D:2 * D], ALU.add))
                vec.tensor_tensor(res[:, m, :, :], res[:, m, :, :], rows[:, m, :, 0:D], ALU.add
                                  ).then_inc(summed.sem, 1)
                dve.wait_ge(summed.sem, summed.at(i))
                for t in range(NT):
                    last = vec.bn_stats(st[:, t, :], res[:, m, t, :])
                chain.step(last)
                carrier.take()
                for t in range(NT):
                    last = vec.bn_aggr(mv[:, m, t, :], st[:, t, :])
                last.then_inc(variance_ready.sem, 1)
                chain.end()

            def norm(i, m, r):
                dve.wait_ge(deviation_ready.sem, deviation_ready.at(i))
                if later(i, CS):
                    dve.wait_ge(stored[m].sem, stored[m].at(r - 1))
                for t in range(NT):
                    last = vec.tensor_scalar(fin[:, m, t, :], res[:, m, t, :], mv[:, m, t, 0:1], mv[:, m, t, 1:2],
                                             ALU.subtract, ALU.mult)
                last.then_inc(normed.sem, 1)

            def step(i, m, r):
                sums(i, m, r)
                if later(i):
                    norm(i - 1, (m - 1) % CS, r + (m - 1) // CS)

            sequences(dve, step)
            norm(nseq - 1, CS - 1, nseq // CS - 1)

        @block.scalar
        def _(act):
            def store(i, m, r):
                act.wait_ge(normed.sem, normed.at(i))
                act.dma_start(out[bass.ds(i * T, T), :].rearrange("(t p) d -> p t d", p=P), fin[:, m, :, :]
                              ).then_inc(stored[m].sem, 16)

            sequences(act, store)
            for m in range(CS):
                act.wait_ge(stored[m].sem, stored[m].at(nseq // CS - 1))


def host_arrays(i):
    def a(name):
        return np.asarray(i[name])

    x = a("L0_attn_x").reshape(-1, D)
    pad = FJ * P - FH
    s_gu = np.stack([np.pad(a(f"L0_ffn_s_{n}"), (0, pad)).reshape(FJ, P).T for n in ("gate", "up")], 1)
    return {
        "x": x, "xT": x.T,
        "w_in": a("L0_attn_W_in"), "w_out": a("L0_attn_W_out"),
        "a_log": np.broadcast_to(a("L0_attn_A_log"), (P, H)),
        "dt_bias": np.broadcast_to(a("L0_attn_dt_bias"), (P, H)),
        "bc_bias": np.broadcast_to(np.concatenate([a("L0_attn_B_norm_bias"), a("L0_attn_C_norm_bias")], 0), (P, 2, N)),
        "w_gate": a("L0_ffn_wq_gate").T, "w_up": a("L0_ffn_wq_up").T, "w_down": a("L0_ffn_wq_down").T,
        "s_gu": s_gu, "s_down": np.broadcast_to(a("L0_ffn_s_down"), (P, D)),
        "w_qkv": a("L1_attn_w_qkv").T, "w_sw": a("L1_attn_w_swiglu").T, "w_so": a("L1_attn_w_out").T,
        "w_route": a("L1_ffn_gate_inp").T,
        "w_ug": np.concatenate([a("L1_ffn_W_up").transpose(0, 2, 1), a("L1_ffn_W_gate").transpose(0, 2, 1)], 2),
        "w_dn": a("L1_ffn_W_down").transpose(0, 2, 1),
        "matrices": constant_matrices(), "small": small_constants(tile_count(x.shape[0])),
    }


def kernel(**inputs):
    import concourse.bacc as _bacc
    from concourse.bass_utils import run_bass_kernel_spmd as _run

    arrays = {f"in_{n}": np.ascontiguousarray(v) for n, v in host_arrays(inputs).items()}
    nc = _bacc.Bacc("TRN2", target_bir_lowering=False, num_devices=1)
    args = {n[3:]: nc.dram_tensor(n, v.shape, mybir.dt.from_np(v.dtype), kind="ExternalInput").ap()
            for n, v in arrays.items()}
    shape = np.asarray(inputs["L0_attn_x"]).shape
    out = nc.dram_tensor("out", [shape[0] * shape[1], D], F32, kind="ExternalOutput").ap()
    build(nc, args, out)
    r = _run(nc, [arrays], core_ids=[0])
    return r.results[0]["out"].reshape(shape)
```
